# Optimizing a Trainium2 kernel written in Bass

```python
import numpy as np
import jax
import jax.numpy as jnp

def _softmax(x, axis=-1):
    return jax.nn.softmax(x, axis=axis)

def _gelu(x):
    return jax.nn.gelu(x, approximate=True)

def _silu(x):
    return jax.nn.silu(x)

def _sigmoid(x):
    return jax.nn.sigmoid(x)

def _layernorm(x, axis=-1, eps=1e-05):
    m = jnp.mean(x, axis=axis, keepdims=True)
    v = jnp.var(x, axis=axis, keepdims=True)
    return (x - m) / jnp.sqrt(v + eps)

def _scatter_add(tgt, idx, src, axis=0):
    return tgt.at[idx].add(src)

def _segment_sum(src, seg, n):
    return jax.ops.segment_sum(src, seg, n)
kernel_name = 'mk_metaformer_d1_conv_nchw512_r2_ff7dfa'

def setup_inputs(seed: int=0):
    np.random.seed(seed)
    _w = jnp.asarray

    def _rec_inputs():
        import jax
        import jax.numpy as jnp
        _gk = jax.random.key(seed)
        x = 7.22e-05 + 1 * jax.random.normal(jax.random.fold_in(_gk, 1), (4, 256, 32, 32), jnp.float32)
        return x
    x = _rec_inputs()

    def _L0_conv_setup():
        import jax, jax.numpy as jnp
        import numpy as np
        from jax import lax
        NUM_HEADS = 4
        NUM_GROUPS = 32
        EPS = 1e-05

        def group_norm(x, gamma, beta):
            b, c, t = x.shape
            xg = x.reshape(b, NUM_GROUPS, c // NUM_GROUPS, t)
            mu = jnp.mean(xg, axis=(2, 3), keepdims=True)
            var = jnp.var(xg, axis=(2, 3), keepdims=True)
            xg = (xg - mu) * lax.rsqrt(var + EPS)
            x = xg.reshape(b, c, t)
            return x * gamma[None, :, None] + beta[None, :, None]

        def conv1d_same(x, w, b):
            k = w.shape[-1]
            left = (k - 1) // 2
            right = k - 1 - left
            y = lax.conv_general_dilated(x, w, window_strides=(1,), padding=[(left, right)], dimension_numbers=('NCH', 'OIH', 'NCH'))
            return y + b[None, :, None]

        def qkv_attention(qkv):
            ch = qkv.shape[1] // 3
            q, k, v = jnp.split(qkv, 3, axis=1)
            scale = float(ch) ** (-0.25)
            w = jnp.einsum('bct,bcs->bts', q * scale, k * scale)
            w = jax.nn.softmax(w.astype(jnp.float32), axis=-1).astype(qkv.dtype)
            return jnp.einsum('bts,bcs->bct', w, v)
        key = jax.random.key(seed)
        ks = jax.random.split(key, 5)
        B, C, H, W = (4, 256, 32, 32)
        x = jax.random.normal(ks[0], (B, C, H, W), dtype=jnp.float32)
        gn_gamma = jnp.ones((C,), dtype=jnp.float32)
        gn_beta = jnp.zeros((C,), dtype=jnp.float32)
        qkv_w = jax.random.normal(ks[1], (3 * C, C, C // 16), dtype=jnp.float32) * 0.02
        qkv_b = jax.random.normal(ks[2], (3 * C,), dtype=jnp.float32) * 0.02
        proj_w = jax.random.normal(ks[3], (C, C, 5), dtype=jnp.float32) * 0.02
        proj_b = jax.random.normal(ks[4], (C,), dtype=jnp.float32) * 0.02
        return {'x': x, 'gn_gamma': gn_gamma, 'gn_beta': gn_beta, 'qkv_w': qkv_w, 'qkv_b': qkv_b, 'proj_w': proj_w, 'proj_b': proj_b}
    _L0_conv_all = _L0_conv_setup()
    _L0_conv_in = {k: v for k, v in _L0_conv_all.items() if k in ('gn_gamma', 'gn_beta', 'qkv_w', 'qkv_b', 'proj_w', 'proj_b')}
    del _L0_conv_all

    def _L0_ffn_setup():
        import jax, jax.numpy as jnp
        import numpy as np
        MARK_AX = 0
        OPCODE_BASE = 16
        OP_SHL = OPCODE_BASE + 23
        OP_SHR = OPCODE_BASE + 24
        ALU_LO = 32
        ALU_HI = 40
        AX_CARRY_LO = 48
        OUTPUT_LO = 64
        OUTPUT_HI = 72
        B, SEQ, D = (8, 16384, 256)
        key = jax.random.key(seed)
        ks = jax.random.split(key, 6)
        x = jax.random.uniform(ks[0], (B, SEQ, D), dtype=jnp.float32) * 0.4
        mark = (jax.random.uniform(ks[1], (B, SEQ)) < 0.75).astype(jnp.float32)
        op_sel = jax.random.randint(ks[2], (B, SEQ), 0, 3)
        lo = jax.random.randint(ks[3], (B, SEQ), 0, 16)
        hi = jax.random.randint(ks[4], (B, SEQ), 0, 16)
        sa = jax.random.randint(ks[5], (B, SEQ), 0, 16)
        oh = lambda idx: jax.nn.one_hot(idx, 16, dtype=jnp.float32)
        x = x.at[..., MARK_AX].set(mark)
        x = x.at[..., OP_SHL].set((op_sel == 1).astype(jnp.float32))
        x = x.at[..., OP_SHR].set((op_sel == 2).astype(jnp.float32))
        x = x.at[..., ALU_LO:ALU_LO + 16].set(oh(lo))
        x = x.at[..., ALU_HI:ALU_HI + 16].set(oh(hi))
        x = x.at[..., AX_CARRY_LO:AX_CARRY_LO + 16].set(oh(sa))
        return {'x_bd': x}
    _L0_ffn_all = _L0_ffn_setup()
    _L0_ffn_in = {k: v for k, v in _L0_ffn_all.items() if k in ()}
    del _L0_ffn_all
    return {'x': x, 'L0_conv_gn_gamma': _L0_conv_in['gn_gamma'], 'L0_conv_gn_beta': _L0_conv_in['gn_beta'], 'L0_conv_qkv_w': _L0_conv_in['qkv_w'], 'L0_conv_qkv_b': _L0_conv_in['qkv_b'], 'L0_conv_proj_w': _L0_conv_in['proj_w'], 'L0_conv_proj_b': _L0_conv_in['proj_b']}

def reference(x, L0_conv_gn_gamma, L0_conv_gn_beta, L0_conv_qkv_w, L0_conv_qkv_b, L0_conv_proj_w, L0_conv_proj_b):
    import jax
    import jax.numpy as jnp

    def _L0_conv_ref(x, gn_gamma, gn_beta, qkv_w, qkv_b, proj_w, proj_b):
        import jax, jax.numpy as jnp
        import numpy as np
        from jax import lax
        NUM_HEADS = 4
        NUM_GROUPS = 32
        EPS = 1e-05

        def group_norm(x, gamma, beta):
            b, c, t = x.shape
            xg = x.reshape(b, NUM_GROUPS, c // NUM_GROUPS, t)
            mu = jnp.mean(xg, axis=(2, 3), keepdims=True)
            var = jnp.var(xg, axis=(2, 3), keepdims=True)
            xg = (xg - mu) * lax.rsqrt(var + EPS)
            x = xg.reshape(b, c, t)
            return x * gamma[None, :, None] + beta[None, :, None]

        def conv1d_same(x, w, b):
            k = w.shape[-1]
            left = (k - 1) // 2
            right = k - 1 - left
            y = lax.conv_general_dilated(x, w, window_strides=(1,), padding=[(left, right)], dimension_numbers=('NCH', 'OIH', 'NCH'))
            return y + b[None, :, None]

        def qkv_attention(qkv):
            ch = qkv.shape[1] // 3
            q, k, v = jnp.split(qkv, 3, axis=1)
            scale = float(ch) ** (-0.25)
            w = jnp.einsum('bct,bcs->bts', q * scale, k * scale)
            w = jax.nn.softmax(w.astype(jnp.float32), axis=-1).astype(qkv.dtype)
            return jnp.einsum('bts,bcs->bct', w, v)
        b, c = (x.shape[0], x.shape[1])
        spatial = x.shape[2:]
        t = int(np.prod(spatial))
        xf = x.reshape(b, c, t)
        qkv = conv1d_same(group_norm(xf, gn_gamma, gn_beta), qkv_w, qkv_b)
        qkv = qkv.reshape(b * NUM_HEADS, -1, t)
        h = qkv_attention(qkv)
        h = h.reshape(b, -1, t)
        h = conv1d_same(h, proj_w, proj_b)
        return (xf + h).reshape(b, c, *spatial)

    def _L0_ffn_ref(x_bd):
        import jax, jax.numpy as jnp
        import numpy as np
        MARK_AX = 0
        OPCODE_BASE = 16
        OP_SHL = OPCODE_BASE + 23
        OP_SHR = OPCODE_BASE + 24
        ALU_LO = 32
        ALU_HI = 40
        AX_CARRY_LO = 48
        OUTPUT_LO = 64
        OUTPUT_HI = 72
        B, SEQ, D = (8, 16384, 256)
        hot = x_bd > 0.5
        first16 = lambda off: jnp.argmax(hot[..., off:off + 16], axis=-1).astype(jnp.int32)
        lo = first16(ALU_LO)
        hi = first16(ALU_HI)
        sa = first16(AX_CARRY_LO)
        val = lo + 16 * hi
        shl = jnp.left_shift(val, sa) & 255
        shr = jnp.right_shift(val, sa)
        mark = hot[..., MARK_AX]
        is_shl = hot[..., OP_SHL]
        is_shr = jnp.logical_and(hot[..., OP_SHR], jnp.logical_not(is_shl))
        act_shl = jnp.logical_and(mark, is_shl)
        act_shr = jnp.logical_and(mark, is_shr)
        active = jnp.logical_or(act_shl, act_shr)
        res = jnp.where(act_shl, shl, jnp.where(act_shr, shr, 0))
        res = jnp.clip(res, 0, 255)
        rlo = res & 15
        rhi = res >> 4
        amp = 2.0 * active.astype(x_bd.dtype)
        add_lo = amp[..., None] * jax.nn.one_hot(rlo, 16, dtype=x_bd.dtype)
        add_hi = amp[..., None] * jax.nn.one_hot(rhi, 16, dtype=x_bd.dtype)
        out = x_bd.at[..., OUTPUT_LO:OUTPUT_LO + 16].add(add_lo)
        out = out.at[..., OUTPUT_HI:OUTPUT_HI + 16].add(add_hi)
        return out

    def _gn(v, G=32, eps=1e-05):
        B_, C_, H_, W_ = v.shape
        g = v.reshape(B_, G, C_ // G, H_, W_)
        m = jnp.mean(g, axis=(2, 3, 4), keepdims=True)
        s = jnp.var(g, axis=(2, 3, 4), keepdims=True)
        return ((g - m) / jnp.sqrt(s + eps)).reshape(v.shape)

    def _ln_c(v, eps=1e-06):
        m = jnp.mean(v, axis=1, keepdims=True)
        s = jnp.var(v, axis=1, keepdims=True)
        return (v - m) / jnp.sqrt(s + eps)

    def _ln_t(v, eps=1e-05):
        m = jnp.mean(v, axis=-1, keepdims=True)
        s = jnp.var(v, axis=-1, keepdims=True)
        return (v - m) / jnp.sqrt(s + eps)

    def _to_tokens(v):
        B_, C_, H_, W_ = v.shape
        return v.reshape(B_, C_, H_ * W_).transpose(0, 2, 1)

    def _from_tokens(t, like):
        B_, C_, H_, W_ = like.shape
        return t.transpose(0, 2, 1).reshape(B_, C_, H_, W_)
    x = x + _L0_conv_ref(_ln_c(x), L0_conv_gn_gamma, L0_conv_gn_beta, L0_conv_qkv_w, L0_conv_qkv_b, L0_conv_proj_w, L0_conv_proj_b)
    t = _to_tokens(x)
    t = t + _L0_ffn_ref(_ln_t(t))
    x = _from_tokens(t, x)
    return x

_drawn_inputs = setup_inputs


def setup_inputs(seed=0):
    import zlib

    import numpy as np

    out = dict(_drawn_inputs(seed))
    spreads = {'L0_conv_gn_gamma': (1.0, 0.553), 'L0_conv_gn_beta': (0.0, 0.1)}
    factors = {'L0_conv_qkv_b': 6.799, 'L0_conv_proj_b': 5.306}
    for name, (base, spread) in spreads.items():
        noise = np.random.default_rng([zlib.crc32(name.encode()), seed]).standard_normal(out[name].shape)
        drawn = base * np.exp(spread * noise) if base else spread * noise
        out[name] = jnp.asarray(drawn.astype(out[name].dtype))
    for name, factor in factors.items():
        out[name] = (out[name] * factor).astype(out[name].dtype)
    return out
```

```python
from contextlib import ExitStack

import concourse.bass as bass
from concourse import mybir

F32 = mybir.dt.float32
F16 = mybir.dt.float16
I32 = mybir.dt.int32
ALU = mybir.AluOpType
ACT = mybir.ActivationFunctionType
X = mybir.AxisListType.X
ABSMAX = bass.bass_isa.ReduceOp.absmax

P = 128
NB, T, C = 4, 1024, 256
CT = C // P
HALF = T // 2
TAPS, PTAPS = 16, 5
PH_TAPS = TAPS // 2
PAIRS, TILES = 2, 3
STEPS = PAIRS * NB
D = 64
UNITS = 16
SLOTS = 18
SEQW = HALF + PH_TAPS
HW = HALF + 2
LEFT = 4
EXP23 = float(1 << 23)
PROB_BITS = 13
WK, UK, QK, PK = 13, 13, 14, 14


def build(nc, x_tok, w_qkv, b_qkv, gamma, beta, w_proj, b_proj, ident_in, group_in, ramp_in, out_tok):
    with ExitStack() as ctx:
        def sb(name, shape, dt):
            return ctx.enter_context(nc.sbuf_tensor(name, shape, dt))

        def ps(name, shape):
            return ctx.enter_context(nc.psum_tensor(name, shape, F32))

        def sem(name):
            return ctx.enter_context(nc.semaphore(name))

        W = sb("W", [P, TILES, 2, CT, 3, PH_TAPS, P], F16)
        U = sb("U", [P, 2, CT, NB, 3, SEQW], F16)
        stack = sb("stack", [P, 2, 3, T], F16)
        yv = sb("yv", [P, T], F32)
        yqk = sb("yqk", [P, T], F32)
        m_sb = sb("m_sb", [P, HALF], F32)
        arena = sb("arena", [P, 5 * T], F32)
        prob = arena[:, 0:T]
        probT = arena[:, T:5 * T].bitcast(F16).rearrange("p (l s t) -> p l s t", l=2, s=8)
        eo = arena[:, 0:CT * 2 * SEQW].rearrange("p (c r w) -> p c r w", c=CT, r=2)
        diff = arena[:, CT * 2 * SEQW:2 * CT * 2 * SEQW].rearrange("p (d c w) -> p d c w", d=2, c=CT)
        vT = sb("vT", [P, 8, 2, P], F16)
        hbuf = sb("hbuf", [P, 2, HALF], F32)
        wsum = hbuf[:, :, :].rearrange("p a (b c) -> p (a b) c", c=P)
        H = [sb(f"H{p}", [P, 2, NB, 2, HW], F16) for p in range(PAIRS)]
        xs = H[0][:, :, :, :, :].rearrange("p a b r w -> p (a b r w)")[:, 0:8192].bitcast(F32) \
            .rearrange("p (n i c) -> p n i c", n=2, i=8)
        wst = H[1][:, :, :, :, :].rearrange("p a b r w -> p (a b r w)")[:, 0:8192].bitcast(F32) \
            .rearrange("p (c s k o) -> p c s k o", c=CT, s=2, k=PH_TAPS)
        ident = sb("ident_sb", [P, P], F32)
        group = sb("group_sb", [P, P], F32)
        ln = sb("ln", [P, NB, 8, 2], F32)
        st = sb("st", [P, 8, 6], F32)
        gs = sb("gs", [P, CT, 4], F32)
        gn = sb("gn", [P, CT, 4], F32)
        ab = sb("ab", [P, CT, 2], F32)
        nt = sb("nt", [P, 3, 8], F32)
        par = sb("par", [P, 2, CT], F32)
        qb = sb("qb", [P, 6], F32)
        am = sb("am", [P, 8], F32)
        amr = sb("amr", [P, 8], F32)
        bits = sb("bits", [P, 2], I32)
        usc = sb("usc", [P, 2], F32)
        wsc = sb("wsc", [P, 2, 6], F32)
        isc = sb("isc", [P, 6], F32)
        ysc = sb("ysc", [P, 2], F32)
        vsc = sb("vsc", [P, STEPS], F32)
        vscale = sb("vscale", [P, 1], F32)
        esc = sb("esc", [P, 2, 2], F32)
        smx = sb("smx", [P, 4], F32)
        Wf = W[:, :, :, :, :, :, :].rearrange("p a b c d e f -> p (a b c d e f)")
        Uf = U[:, :, :, :, :, :].rearrange("p a b c d e -> p (a b c d e)")
        PWN = PAIRS * PTAPS * C
        pws = Wf[:, 0:2 * PWN].bitcast(F32)
        pw = Wf[:, 2 * PWN:4 * PWN].rearrange("p (l a k o) -> p l a k o", l=2, a=PAIRS, k=PTAPS)
        x1 = Wf[:, 4 * PWN:4 * PWN + 4096].bitcast(F32).rearrange("p (i c) -> p i c", i=8)
        zz = Wf[:, 4 * PWN + 4096:4 * PWN + 8192].bitcast(F32).rearrange("p (i c) -> p i c", i=8)
        ob = Wf[:, 4 * PWN + 8192:4 * PWN + 16384].bitcast(F32).rearrange("p (n i c) -> p n i c", n=2, i=8)
        xf = Uf[:, 0:8192].bitcast(F32).rearrange("p (n i c) -> p n i c", n=2, i=8)
        base = Uf[:, 8192:16384].bitcast(F32).rearrange("p (n i c) -> p n i c", n=2, i=8)
        pbb = Uf[:, 16384:16896].bitcast(F32)
        hot = Uf[:, 16896:17152].bitcast(F32).rearrange("p (i k) -> p i k", i=8)
        tail = Uf[:, 17152:17152 + 512].bitcast(F32).rearrange("p (f i) -> p f i", i=8)
        taili = Uf[:, 17664:17664 + 256].bitcast(I32).rearrange("p (f i) -> p f i", i=8)
        ramp = sb("ramp_sb", [P, 2, 16], F32)
        alpha = sb("alpha", [P, STEPS], F32)
        pwsc = sb("pwsc", [P, 2], F32)

        bank = [ps("cM", [P, HALF]), ps("cP", [P, HALF]), ps("cQ", [P, HALF])]
        psS = ps("psS", [P, T])
        psT = ps("psT", [P, T])
        psV = ps("psV", [P, HALF])
        pj = [bank[0][:, :], bank[1][:, :], bank[2][:, :], psS[:, 0:HALF], psS[:, HALF:T],
              psT[:, 0:HALF], psT[:, HALF:T], psV[:, :]]

        names = """par_in pads x_in0 x_in1 z_done zT_done gstat_done gmm_done ab_done eo_done diff_done uhi_done
            ulo_done ln_sq ln_var gn_var gn_sq ws_in0 ws_in1 ws_used wam_done war_done wsc_done wsum_done wsum_used whi_done
            bam_done bar_done conv_done m_done y0_done y1_done yam_done yar_done ysc_done
            s_done nb_done e_done pn_done t_done ph_done pl_done pv_done ht_done hs_done hh_done hl_done
            vt_done vh_done vl_done qk_hi qk_done pw_in pwam_done pwar_done pwsc_done pwhi_done pw_done
            xf_in0 xf_in1 xf_used zf_done base_done pj_done pj_used f_var f_sq o_sum zz_done o_done out_sent0 out_sent1
            c_a c_b c_g c_w c_u c_y c_s c_h c_k c_f c_p c_z""".split()
        S = {n: sem(n) for n in names}

        class Chain:
            def __init__(self, eng, name, run, per_run):
                self.eng, self.sem, self.start, self.per_run, self.n = eng, S[name], run * per_run, per_run, 0

            def done(self, ins):
                ins.then_inc(self.sem, 1)
                self.n += 1

            def wait(self):
                self.eng.wait_ge(self.sem, self.start + self.n)

            def step(self, ins):
                self.done(ins)
                self.wait()

            def end(self):
                assert self.n == self.per_run, (self.sem, self.n, self.per_run)

        def pow2(ch, src, k, scale, inverse):
            v = nc.vector
            ch.step(v.tensor_scalar(inverse, src, 1e-30, None, ALU.max))
            ch.step(v.tensor_scalar(bits[:, 0:1], inverse.bitcast(I32), 0x7F800000, None, ALU.bitwise_and))
            ch.done(v.tensor_scalar(scale.bitcast(I32), bits[:, 0:1], -1.0, (254 + k) * EXP23, ALU.mult, ALU.add))
            ch.step(v.tensor_scalar(inverse.bitcast(I32), bits[:, 0:1], 1.0, -k * EXP23, ALU.mult, ALU.add))

        def rstd(ch, eng, var, eps, out, sq_asked, sq_done, runs):
            v = nc.vector
            n = nt[:, 0, 0:var.shape[-1]]
            s = nt[:, 1, 0:var.shape[-1]]
            q = nt[:, 2, 0:var.shape[-1]]
            v.tensor_scalar(n, var, eps, None, ALU.add).then_inc(S[sq_asked], 1)
            eng.wait_ge(S[sq_done], runs)
            ch.step(v.reciprocal(q, s))
            ch.step(v.tensor_tensor(s, n, q, ALU.mult))
            ch.step(v.tensor_tensor(s, s, q, ALU.mult))
            ch.step(v.tensor_scalar(s, s, -0.5, 1.5, ALU.mult, ALU.add))
            ch.step(v.tensor_tensor(out, q, s, ALU.mult))

        PE0 = {3: ("zT", 1), 5: ("gmm", 1), 8: ("zT", 2), 10: ("gmm", 2), 13: ("zT", 3), 15: ("gmm", 3)}
        EX0 = {0: ("ln", 1), 1: ("w", 1), 4: ("gn", 1), 5: ("ln", 2), 6: ("w", 2), 9: ("gn", 2), 10: ("ln", 3),
               14: ("gn", 3)}

        def is_int(v):
            return isinstance(v, int)

        def wait(eng, name, value):
            if not (is_int(value) and value <= 0):
                eng.wait_ge(S[name], value)

        def pa(n, p):
            return p - 1 if is_int(n) and n % NB == 0 else p

        def ba(n, b):
            return NB - 1 if is_int(n) else b - 1

        block = ctx.enter_context(nc.Block())

        @block.sync
        def _(sp):
            xv = x_tok.rearrange("b (j p r) c -> b p j (r c)", j=4, r=2)
            ov = out_tok.rearrange("b (j p r) c -> b p j (r c)", j=4, r=2)

            def load_x(b):
                if b >= 2:
                    sp.wait_ge(S["zT_done"], b - 1)
                sp.dma_start(xs[:, b % 2, :, :].rearrange("p (j r) c -> p j (r c)", r=2), xv[b]) \
                    .then_inc(S[f"x_in{b % 2}"], 16)

            def load_w(m):
                if m >= 1:
                    sp.wait_ge(S["ws_used"], m)
                    sp.wait_ge(S["whi_done"], 4 * m)
                for c in range(CT):
                    sp.dma_start(wst[:, c].rearrange("p s k o -> p (s k o)"), w_qkv[m, c]).then_inc(S[f"ws_in{c}"], 16)

            for dst, src in ((par[:, 0, :], gamma), (par[:, 1, :], beta), (qb[:, :], b_qkv), (ident[:, :], ident_in),
                             (group[:, :], group_in), (ramp[:, :, :].rearrange("p a b -> p (a b)"), ramp_in)):
                sp.dma_start(dst, src).then_inc(S["par_in"], 16)
            load_x(0)
            load_w(0)
            load_x(1)
            load_w(1)
            load_x(2)
            load_w(2)
            load_x(3)
            for m in range(3, 6):
                load_w(m)
            sp.wait_ge(S["conv_done"], 9 * STEPS)
            sp.dma_start(pws, w_proj).then_inc(S["pw_in"], 16)
            sp.dma_start(pbb, b_proj.to_broadcast([P, C])).then_inc(S["pw_in"], 16)
            for b in range(NB):
                if b >= 2:
                    sp.wait_ge(S["base_done"], b - 1)
                sp.dma_start(xf[:, b % 2, :, :].rearrange("p (j r) c -> p j (r c)", r=2), xv[b]) \
                    .then_inc(S[f"xf_in{b % 2}"], 16)
            for b in range(NB):
                sp.wait_ge(S["o_done"], b + 1)
                sp.dma_start(ov[b], ob[:, b % 2, :, :].rearrange("p (j r) c -> p j (r c)", r=2)) \
                    .then_inc(S[f"out_sent{b % 2}"], 16)
            sp.wait_ge(S["out_sent0"], 32)
            sp.wait_ge(S["out_sent1"], 32)

        @block.gpsimd
        def _(pool):
            g = nc.gpsimd

            def weights(m):
                pool.wait_ge(S["wam_done"], m + 1)
                g.partition_all_reduce(amr[:, 0:1], am[:, 0:1], P, ABSMAX).then_inc(S["war_done"], 1)
                for c in range(CT):
                    wait(pool, "wsum_used", 2 * m + c)
                    pool.wait_ge(S[f"ws_in{c}"], 16 * (m + 1))
                    g.tensor_tensor(wsum, wst[:, c, 0], wst[:, c, 1], ALU.add).then_inc(S["wsum_done"], 1)

            def group_norm(b):
                pool.wait_ge(S["eo_done"], 4 * (b + 1))
                wait(pool, "ulo_done", 3 * b)
                for d in range(2):
                    g.tensor_tensor(diff[:, d, :, 0:SEQW - 1], eo[:, :, 1, d:d + SEQW - 1], eo[:, :, 0, 1:SEQW],
                                    ALU.subtract).then_inc(S["diff_done"], 1)

            def amax(run):
                pool.wait_ge(S["yam_done"], run + 1)
                g.tensor_tensor(am[:, 6:7], am[:, 2:3], ramp[:, 1, 1:2], ALU.mult)
                pool.drain()
                g.partition_all_reduce(amr[:, 2:3], am[:, 6:7], P, ABSMAX).then_inc(S["yar_done"], 1)

            pool.wait_ge(S["bam_done"], 1)
            g.partition_all_reduce(amr[:, 1:2], am[:, 1:2], P, ABSMAX).then_inc(S["bar_done"], 1)
            g.memset(eo[:, :, :, 0:LEFT], 0.0).then_inc(S["pads"], 1)
            g.memset(eo[:, :, :, LEFT + HALF:SEQW], 0.0).then_inc(S["pads"], 1)
            weights(0)
            group_norm(0)

            def step(n, attn, extra):
                for i in range(SLOTS):
                    if extra and i in EX0:
                        kind, k = EX0[i]
                        if kind == "w":
                            weights(k)
                        if kind == "gn":
                            group_norm(k)
                    if attn and i == 0:
                        amax(3 * n - 1)
                    if i == 6:
                        amax(3 * n)
                    if i == 12:
                        amax(3 * n + 1)

            step(0, False, True)
            with pool.Fori(1, NB) as n:
                step(n, True, False)
            for m in range(3, 6):
                weights(m)
            pool.wait_ge(S["wsum_used"], 12)
            for p in range(PAIRS):
                for e in (0, HW - 1):
                    g.memset(H[p][:, :, :, :, e:e + 1].rearrange("p a b r w -> p (a b r) w"), 0.0).then_inc(S["pads"], 1)
            step(NB, True, False)
            with pool.Fori(NB + 1, STEPS) as n:
                step(n, True, False)
            amax(3 * STEPS - 1)
            pool.wait_ge(S["pwam_done"], 1)
            g.partition_all_reduce(amr[:, 3:4], am[:, 3:4], P, ABSMAX).then_inc(S["pwar_done"], 1)
            pool.wait_ge(S["pw_in"], 32)
            def out_sum(b):
                pool.wait_ge(S["zz_done"], 8 * (b + 1))
                if b >= 2:
                    pool.wait_ge(S[f"out_sent{b % 2}"], 16)
                g.tensor_tensor(ob[:, b % 2], x1, zz, ALU.add).then_inc(S["o_sum"], 1)

            for b in range(NB):
                pool.wait_ge(S["zf_done"], 8 * (b + 1))
                g.tensor_tensor(base[:, b % 2], base[:, b % 2], xf[:, b % 2], ALU.add).then_inc(S["c_z"], 1)
                pool.wait_ge(S["c_z"], b + 1)
                g.tensor_tensor(base[:, b % 2], base[:, b % 2], pbb[:, :].rearrange("p (o c) -> p o c", o=1)
                                .to_broadcast([P, 8, C]), ALU.add).then_inc(S["base_done"], 1)
                if b >= 1:
                    out_sum(b - 1)
            out_sum(NB - 1)

        @block.scalar
        def _(act):
            a = nc.scalar.activation

            def sqrt(asked, done, runs, width):
                act.wait_ge(S[asked], runs)
                a(nt[:, 1, 0:width], nt[:, 0, 0:width], ACT.Sqrt).then_inc(S[done], 1)

            def weights(m):
                j = m % 3
                act.wait_ge(S["wsc_done"], m + 1)
                if m >= 3:
                    act.wait_ge(S["conv_done"], 27 + 3 * j + 3)
                for c in range(CT):
                    a(W[:, j, 0, c, 1:3], wst[:, c], ACT.Copy, scale=wsc[:, 0, m:m + 1]).then_inc(S["whi_done"], 1)
                    act.wait_ge(S["wsum_done"], 2 * m + c + 1)
                    a(W[:, j, 0, c, 0], wsum, ACT.Copy, scale=wsc[:, 0, m:m + 1]).then_inc(S["whi_done"], 1)

            def group_norm(b):
                sqrt("gn_var", "gn_sq", b + 1, CT)
                act.wait_ge(S["ab_done"], b + 1)
                act.wait_ge(S["pads"], 2)
                wait(act, "ulo_done", 3 * b)
                for c, src in ((0, psS), (1, psT)):
                    for r in range(2):
                        a(eo[:, c, r, LEFT:LEFT + HALF], src[:, r * HALF:(r + 1) * HALF], ACT.Identity,
                          bias=ab[:, c, 1:2], scale=ab[:, c, 0:1]).then_inc(S["eo_done"], 1)
                act.wait_ge(S["eo_done"], 4 * (b + 1))
                a(U[:, 0, :, b, 0, 0:SEQW - 1], eo[:, :, 0, 1:SEQW], ACT.Copy).then_inc(S["uhi_done"], 1)
                for d in range(2):
                    act.wait_ge(S["diff_done"], 2 * b + d + 1)
                    a(U[:, 0, :, b, 1 + d, 0:SEQW - 1], diff[:, d, :, 0:SEQW - 1], ACT.Copy) \
                        .then_inc(S["uhi_done"], 1)

            def qk_hi(run, hd):
                act.wait_ge(S["ysc_done"], run + 1)
                a(stack[0:D, hd, 0, :], yqk[0:D, :], ACT.Copy, scale=ysc[0:D, 0:1]).then_inc(S["qk_hi"], 1)
                a(stack[D:P, hd, 1, :], yqk[D:P, :], ACT.Copy, scale=ysc[D:P, 0:1]).then_inc(S["qk_hi"], 1)

            def step(n, p, b, attn, conv, extra):
                k = n - 1
                for i in range(SLOTS):
                    if extra and i in EX0:
                        kind, e = EX0[i]
                        if kind == "ln":
                            sqrt("ln_var", "ln_sq", e + 1, 8)
                        if kind == "w":
                            weights(e)
                        if kind == "gn":
                            group_norm(e)
                    if attn and i == 0:
                        act.wait_ge(S["vt_done"], k + 1)
                        act.wait_ge(S["ysc_done"], 3 * k + 1)
                        vt = psT[:, :].rearrange("p (s h c) -> p s h c", s=8, h=2)
                        a(vT[:, :, 0, 0:D], vt[:, :, 0, :], ACT.Copy, scale=vscale[:, 0:1]).then_inc(S["vh_done"], 1)
                        a(vT[:, :, 1, D:P], vt[:, :, 1, :], ACT.Copy, scale=vscale[:, 0:1]).then_inc(S["vh_done"], 1)
                    if attn and 1 <= i <= UNITS:
                        u = i - 1
                        act.wait_ge(S["t_done"], 16 * k + u + 1)
                        if u >= 4:
                            act.wait_ge(S["pv_done"], 4 * k + u // 4)
                        a(probT[:, 0, :, u % 4 * P:(u % 4 + 1) * P], psT[:, :].rearrange("p (s t) -> p s t", s=8),
                          ACT.Copy).then_inc(S["ph_done"], 1)
                    if attn and i < UNITS:
                        u, hd = i, i // 8
                        act.wait_ge(S["nb_done"], 16 * k + u + 1)
                        if u:
                            act.wait_ge(S["t_done"], 16 * k + u)
                        a(prob, psS[:, :], ACT.Exp, bias=smx[:, 1:2], scale=esc[:, hd, 0:1],
                          accum_out=smx[:, 2:3]).then_inc(S["e_done"], 1)
                    if conv and i in (2, 8, 14):
                        j = i // 6
                        act.wait_ge(S["conv_done"], 9 * n + 3 * j + 1)
                        wait(act, "y1_done", 3 * n + j)
                        a(m_sb[:, :], bank[0][:, :], ACT.Identity, bias=qb[:, 3 * p + j:3 * p + j + 1],
                          scale=isc[:, 3 * p + j:3 * p + j + 1]).then_inc(S["m_done"], 1)
                    if attn and i == 1:
                        qk_hi(3 * k + 2, 1)
                    if conv and i == 13:
                        qk_hi(3 * n + 1, 0)
                    if attn and i in (5, 9, 13, 17):
                        gi = (i - 5) // 4
                        hd, r = gi // 2, gi % 2
                        R, O = D * hd, D * (1 - hd)
                        act.wait_ge(S["pv_done"], 4 * k + gi + 1)
                        a(hbuf[R:R + D, 0, :], psV[O:O + D, :], ACT.Copy, scale=2.0 ** -PROB_BITS) \
                            .then_inc(S["ht_done"], 1)
                        act.wait_ge(S["hs_done"], 4 * k + gi + 1)
                        a(H[pa(n, p)][R:R + D, 0, ba(n, b), r, 1:1 + HALF], hbuf[R:R + D, 1, :], ACT.Copy) \
                            .then_inc(S["hh_done"], 1)

            sqrt("ln_var", "ln_sq", 1, 8)
            weights(0)
            group_norm(0)
            step(0, 0, 0, False, True, True)
            with act.Fori(1, NB) as n:
                step(n, 0, n, True, True, False)
            for m in range(3, 6):
                weights(m)
            step(NB, 1, 0, True, True, False)
            with act.Fori(NB + 1, STEPS) as n:
                step(n, 1, n - NB, True, True, False)
            step(STEPS, 2, 0, True, False, False)
            act.wait_ge(S["pwsc_done"], 1)
            a(pw[:, 0].rearrange("p a k o -> p (a k o)"), pws, ACT.Copy, scale=pwsc[:, 0:1]).then_inc(S["pwhi_done"], 1)
            for b in range(NB):
                sqrt("f_var", "f_sq", b + 1, 8)

        @block.tensor
        def _(pe):
            mm, tr = nc.tensor.matmul, nc.tensor.transpose

            batch_reg = pe.alloc_register("batch")

            def fresh(b):
                if is_int(b):
                    return b
                pe.reg_mov(batch_reg, b)
                return pe.snap(batch_reg)

            def z_transpose(b):
                pe.wait_ge(S["z_done"], 8 * (b + 1))
                wait(pe, "eo_done", 4 * b)
                for i in range(8):
                    j, r = i // 2, i % 2
                    for c, dst in ((0, psS), (1, psT)):
                        last = tr(dst[:, r * HALF + j * P:r * HALF + (j + 1) * P], xs[:, b % 2, i, c * P:(c + 1) * P],
                                  ident[:, :])
                last.then_inc(S["zT_done"], 1)

            def group_mean(b):
                pe.wait_ge(S["gstat_done"], b + 1)
                mm(psV[:, 0:2 * CT], group[:, :], gs[:, :, 0:2].rearrange("p c k -> p k c"), start=True, stop=True) \
                    .then_inc(S["gmm_done"], 1)

            def step(n, p, b, attn, conv, extra):
                k = n - 1
                for i in range(SLOTS):
                    if extra and i in PE0:
                        (z_transpose if PE0[i][0] == "zT" else group_mean)(PE0[i][1])
                    if attn and i in (5, 9, 13, 17):
                        gi = (i - 5) // 4
                        hd = gi // 2
                        pe.wait_ge(S["pl_done"], 16 * k + 4 * gi + 4)
                        if gi == 0:
                            pe.wait_ge(S["vl_done"], 2 * k + 2)
                        if gi:
                            pe.wait_ge(S["hs_done"], 4 * k + gi)
                        for s in range(8):
                            for l in range(2):
                                last = mm(psV[:, :], vT[:, s, hd, :], probT[:, l, s, :], start=(s + l == 0),
                                          stop=(s + l == 8))
                        last.then_inc(S["pv_done"], 1)
                    if attn and 1 <= i <= UNITS:
                        u = i - 1
                        pe.wait_ge(S["pn_done"], 16 * k + u + 1)
                        if u == 0:
                            pe.wait_ge(S["vl_done"], 2 * k + 2)
                        else:
                            pe.wait_ge(S["pl_done"], 16 * k + u)
                        for s in range(8):
                            last = tr(psT[:, s * P:(s + 1) * P], prob[:, s * P:(s + 1) * P], ident[:, :])
                        last.then_inc(S["t_done"], 1)
                    if attn and i < UNITS:
                        u, hd = i, i // 8
                        if u % 8 == 0:
                            pe.wait_ge(S["qk_done"], 2 * k + hd + 1)
                        if u:
                            pe.wait_ge(S["e_done"], 16 * k + u)
                        for h in range(2):
                            for l in range(2):
                                last = mm(psS[:, h * HALF:(h + 1) * HALF], stack[:, hd, 0, u % 8 * P:(u % 8 + 1) * P],
                                          stack[:, hd, 1 + l, h * HALF:(h + 1) * HALF], start=(l == 0), stop=(l == 1))
                        last.then_inc(S["s_done"], 1)
                    if conv:
                        q = i // 2
                        j, kind = q // 3, q % 3
                        if i % 2 == 0:
                            wait(pe, ("m_done", "y0_done", "y1_done")[kind], 3 * n + j)
                            if kind == 0:
                                pe.wait_ge(S["wsum_used"], 2 * (3 * p + j + 1))
                            if i == 0:
                                pe.wait_ge(S["ulo_done"], 3 if extra else 3 * NB)
                        c = i % 2
                        bb = fresh(b)
                        for t in range(PH_TAPS):
                            for wl, ul in ((0, 0), (0, 1), (1, 0)):
                                last = mm(bank[kind][:, :], W[:, j, wl, c, kind, t, :], U[:, ul, c, bb, kind, t:t + HALF],
                                          start=(c == 0 and t == 0 and wl + ul == 0),
                                          stop=(c == 1 and t == PH_TAPS - 1 and wl == 1))
                        if i % 2 == 1:
                            last.then_inc(S["conv_done"], 1)
                if conv:
                    pe.wait_ge(S["y1_done"], 3 * n + 1)
                    if attn:
                        pe.wait_ge(S["pl_done"], 16 * n)
                    else:
                        pe.wait_ge(S["eo_done"], 4 * NB)
                    for s in range(8):
                        last = tr(psT[:, s * P:(s + 1) * P], yv[:, s * P:(s + 1) * P], ident[:, :])
                    last.then_inc(S["vt_done"], 1)

            pe.wait_ge(S["par_in"], 96)
            z_transpose(0)
            group_mean(0)
            step(0, 0, 0, False, True, True)
            with pe.Fori(1, NB) as n:
                step(n, 0, n, True, True, False)
            step(NB, 1, 0, True, True, False)
            with pe.Fori(NB + 1, STEPS) as n:
                step(n, 1, n - NB, True, True, False)
            step(STEPS, 2, 0, True, False, False)
            pe.wait_ge(S["hl_done"], 4 * STEPS)
            pe.wait_ge(S["pw_done"], 1)
            pe.wait_ge(S["pads"], 6)
            def project(b):
                for i in range(8):
                    j, r = i // 2, i % 2
                    bb = fresh(b)
                    wait(pe, "pj_used", b * 8)
                    for p in range(PAIRS):
                        for t in range(PTAPS):
                            d = r + t - 2
                            col = 1 + d // 2 + j * P
                            for hl, wl in ((0, 0), (0, 1), (1, 0)):
                                last = mm(pj[i][:, p * C:(p + 1) * C], H[p][:, hl, bb, d % 2, col:col + P],
                                          pw[:, wl, p, t, :], start=(t == 0 and hl + wl == 0),
                                          stop=(t == PTAPS - 1 and hl == 1), skip_group_check=True)
                    last.then_inc(S["pj_done"], 1)

            project(0)
            with pe.Fori(1, NB) as b:
                project(b)

        @block.vector
        def _(dve):
            v = nc.vector

            def layer_norm_stats(ch, src, dst):
                for i in range(8):
                    ch.done(v.bn_stats(st[:, i, :], src[:, i, :]))
                ch.wait()
                for i in range(8):
                    ch.done(v.bn_aggr(dst[:, i, :], st[:, i, :]))
                ch.wait()

            def layer_norm(b):
                ch = Chain(dve, "c_a", b, 21)
                dve.wait_ge(S[f"x_in{b % 2}"], 16 * (b // 2 + 1))
                layer_norm_stats(ch, xs[:, b % 2], ln[:, b])
                rstd(ch, dve, ln[:, b, :, 1], 1e-6, ln[:, b, :, 1], "ln_var", "ln_sq", b + 1)
                ch.end()
                for i in range(8):
                    v.tensor_scalar(xs[:, b % 2, i, :], xs[:, b % 2, i, :], ln[:, b, i, 0:1], ln[:, b, i, 1:2],
                                    ALU.subtract, ALU.mult).then_inc(S["z_done"], 1)

            def group_norm(b):
                ch = Chain(dve, "c_g", b, 19)
                dve.wait_ge(S["zT_done"], b + 1)
                for c, src in ((0, psS), (1, psT)):
                    for r in range(2):
                        ch.done(v.bn_stats(st[:, 2 * c + r, :], src[:, r * HALF:(r + 1) * HALF]))
                ch.wait()
                for c in range(CT):
                    ch.done(v.bn_aggr(gs[:, c, 0:2], st[:, 2 * c:2 * c + 2, :].rearrange("p a b -> p (a b)")))
                ch.wait()
                ch.step(v.tensor_tensor(gs[:, :, 2], gs[:, :, 0], gs[:, :, 0], ALU.mult))
                v.tensor_tensor(gs[:, :, 1], gs[:, :, 1], gs[:, :, 2], ALU.add).then_inc(S["gstat_done"], 1)
                dve.wait_ge(S["gmm_done"], b + 1)
                ch.step(v.tensor_copy(gn[:, :, 0:2].rearrange("p c k -> p k c"),
                                      psV[:, 0:2 * CT].rearrange("p (k c) -> p k c", k=2)))
                ch.step(v.tensor_tensor(gn[:, :, 2], gn[:, :, 0], gn[:, :, 0], ALU.mult))
                ch.step(v.tensor_tensor(gn[:, :, 3], gn[:, :, 1], gn[:, :, 2], ALU.subtract))
                rstd(ch, dve, gn[:, :, 3], 1e-5, gn[:, :, 1], "gn_var", "gn_sq", b + 1)
                ch.step(v.tensor_tensor(gn[:, :, 1], gn[:, :, 1], par[:, 0, :], ALU.mult))
                ch.step(v.tensor_tensor(gn[:, :, 2], gn[:, :, 0], gn[:, :, 1], ALU.mult))
                ch.step(v.tensor_tensor(gn[:, :, 2], par[:, 1, :], gn[:, :, 2], ALU.subtract))
                wait(dve, "eo_done", 4 * b)
                ch.done(v.tensor_scalar(ab[:, :, 0], gn[:, :, 1], usc[:, 0:1], None, ALU.mult))
                v.tensor_scalar(ab[:, :, 1], gn[:, :, 2], usc[:, 0:1], None, ALU.mult).then_inc(S["ab_done"], 1)
                ch.end()
                for q in range(3):
                    dve.wait_ge(S["uhi_done"], 3 * b + q + 1)
                    if q:
                        dve.wait_ge(S["diff_done"], 2 * b + q)
                    src = eo[:, :, 0, 1:SEQW] if q == 0 else diff[:, q - 1, :, 0:SEQW - 1]
                    v.tensor_tensor(U[:, 1, :, b, q, 0:SEQW - 1], src, U[:, 0, :, b, q, 0:SEQW - 1], ALU.subtract) \
                        .then_inc(S["ulo_done"], 1)

            def weights(m):
                j = m % 3
                ch = Chain(dve, "c_w", m, 6)
                for c in range(CT):
                    dve.wait_ge(S[f"ws_in{c}"], 16 * (m + 1))
                    ch.done(v.tensor_reduce(am[:, 4 + c:5 + c], wst[:, c].rearrange("p s k o -> p (s k o)"), X, ALU.max,
                                            apply_absolute_value=True))
                ch.wait()
                v.tensor_tensor(am[:, 0:1], am[:, 4:5], am[:, 5:6], ALU.max).then_inc(S["wam_done"], 1)
                dve.wait_ge(S["war_done"], m + 1)
                pow2(ch, amr[:, 0:1], WK, wsc[:, 0, m:m + 1], wsc[:, 1, m:m + 1])
                v.tensor_tensor(isc[:, m:m + 1], wsc[:, 1, m:m + 1], usc[:, 1:2], ALU.mult).then_inc(S["wsc_done"], 1)
                ch.end()
                for c in range(CT):
                    dve.wait_ge(S["whi_done"], 4 * m + 2 * c + 1)
                    if m >= 3 and c == 0:
                        dve.wait_ge(S["conv_done"], 27 + 3 * j + 3)
                    last = v.scalar_tensor_tensor(W[:, j, 1, c, 1:3].rearrange("p s k o -> p (s k o)"),
                                                  wst[:, c].rearrange("p s k o -> p (s k o)"), wsc[:, 0, m:m + 1],
                                                  W[:, j, 0, c, 1:3].rearrange("p s k o -> p (s k o)"), ALU.mult,
                                                  ALU.subtract)
                    if c == 1:
                        last.then_inc(S["ws_used"], 1)
                    dve.wait_ge(S["whi_done"], 4 * m + 2 * c + 2)
                    last = v.scalar_tensor_tensor(W[:, j, 1, c, 0], wsum, wsc[:, 0, m:m + 1], W[:, j, 0, c, 0],
                                                  ALU.mult, ALU.subtract)
                    last.then_inc(S["wsum_used"], 1)

            def scale_y(run, j, n):
                ch = Chain(dve, ("c_u", "c_y")[j > 0], n if j == 0 else 2 * n + j - 1, 4 if j == 0 else 5)
                dve.wait_ge(S["yar_done"], run + 1)
                if j == 0:
                    pow2(ch, amr[:, 2:3], QK, vscale[:, 0:1], ysc[:, 1:2])
                    v.tensor_copy(vsc[:, bass.ds(n, 1)], ysc[:, 1:2]).then_inc(S["ysc_done"], 1)
                else:
                    pow2(ch, amr[:, 2:3], QK, ysc[:, 0:1], ysc[:, 1:2])
                    ch.step(v.tensor_scalar(esc[:, j - 1, 0:1], ysc[:, 1:2], ysc[:, 1:2], D ** -0.5, ALU.mult, ALU.mult))
                    v.tensor_scalar(esc[:, j - 1, 1:2], esc[:, j - 1, 0:1], -1.0, None, ALU.mult) \
                        .then_inc(S["ysc_done"], 1)
                ch.end()

            def finish_y(n, p, j):
                y = yv if j == 0 else yqk
                dve.wait_ge(S["conv_done"], 9 * n + 3 * j + 3)
                dve.wait_ge(S["m_done"], 3 * n + j + 1)
                v.scalar_tensor_tensor(y[:, HALF:T], bank[2][:, :], isc[:, 3 * p + j:3 * p + j + 1], m_sb[:, :], ALU.mult,
                                       ALU.add).then_inc(S["y1_done"], 1)
                dve.wait_ge(S["y1_done"], 3 * n + j + 1)
                dve.wait_ge(S["y0_done"], 3 * n + j + 1)
                v.tensor_reduce(am[:, 2:3], y[:, :], X, ALU.max, apply_absolute_value=True).then_inc(S["yam_done"], 1)

            def qk_lo(run, hd, runs):
                ch = Chain(dve, "c_k", runs, 3)
                dve.wait_ge(S["qk_hi"], 2 * runs + 2)
                ch.done(v.scalar_tensor_tensor(stack[D:P, hd, 0, :], yqk[0:D, :], ysc[0:D, 0:1], stack[0:D, hd, 0, :],
                                               ALU.mult, ALU.subtract))
                ch.step(v.scalar_tensor_tensor(stack[D:P, hd, 2, :], yqk[D:P, :], ysc[D:P, 0:1], stack[D:P, hd, 1, :],
                                               ALU.mult, ALU.subtract))
                ch.step(v.tensor_copy(stack[0:D, hd, 1, :], stack[D:P, hd, 1, :]))
                v.tensor_copy(stack[0:D, hd, 2, :], stack[D:P, hd, 2, :]).then_inc(S["qk_done"], 1)
                ch.end()

            def step(n, p, b, attn, conv, extra):
                k = n - 1
                for i in range(SLOTS):
                    if extra and i in EX0:
                        kind, e = EX0[i]
                        {"ln": layer_norm, "w": weights, "gn": group_norm}[kind](e)
                    if attn and i == 0:
                        vt = psT[:, :].rearrange("p (s h c) -> p s h c", s=8, h=2)
                        dve.wait_ge(S["vh_done"], 2 * k + 2)
                        for hd in range(2):
                            v.scalar_tensor_tensor(vT[:, :, hd, D * (1 - hd):D * (2 - hd)], vt[:, :, hd, :], vscale[:, 0:1],
                                                   vT[:, :, hd, D * hd:D * (hd + 1)], ALU.mult, ALU.subtract) \
                                .then_inc(S["vl_done"], 1)
                    if attn and 1 <= i <= UNITS:
                        u = i - 1
                        dve.wait_ge(S["ph_done"], 16 * k + u + 1)
                        v.tensor_tensor(probT[:, 1, :, u % 4 * P:(u % 4 + 1) * P],
                                        psT[:, :].rearrange("p (s t) -> p s t", s=8),
                                        probT[:, 0, :, u % 4 * P:(u % 4 + 1) * P], ALU.subtract) \
                            .then_inc(S["pl_done"], 1)
                    if attn and i < UNITS:
                        u, hd = i, i // 8
                        ch = Chain(dve, "c_s", 16 * k + u, 2)
                        dve.wait_ge(S["s_done"], 16 * k + u + 1)
                        ch.step(v.reduce_max(smx[:, 0:1], psS[:, :], X))
                        v.tensor_scalar(smx[:, 1:2], smx[:, 0:1], esc[:, hd, 1:2], None, ALU.mult) \
                            .then_inc(S["nb_done"], 1)
                        dve.wait_ge(S["e_done"], 16 * k + u + 1)
                        ch.step(v.reciprocal(smx[:, 3:4], smx[:, 2:3]))
                        v.tensor_scalar(prob, prob, smx[:, 3:4], 2.0 ** PROB_BITS, ALU.mult, ALU.mult) \
                            .then_inc(S["pn_done"], 1)
                        ch.end()
                    if attn and i == 0:
                        finish_y(k, pa(n, p), 2)
                    if attn and i == 1:
                        scale_y(3 * k + 2, 2, k)
                    if attn and i == 2:
                        qk_lo(3 * k + 2, 1, 2 * k + 1)
                    if conv and i in (4, 10, 16):
                        j = i // 6
                        dve.wait_ge(S["conv_done"], 9 * n + 3 * j + 2)
                        dve.wait_ge(S["m_done"], 3 * n + j + 1)
                        if j == 0:
                            wait(dve, "vt_done", n)
                        else:
                            wait(dve, "qk_hi", 4 * n + 2 * (j - 1))
                        y = yv if j == 0 else yqk
                        v.scalar_tensor_tensor(y[:, 0:HALF], bank[1][:, :], isc[:, 3 * p + j:3 * p + j + 1], m_sb[:, :],
                                               ALU.mult, ALU.add).then_inc(S["y0_done"], 1)
                    if conv and i in (6, 12):
                        finish_y(n, p, i // 6 - 1)
                    if conv and i in (7, 13):
                        scale_y(3 * n + i // 6 - 1, i // 6 - 1, n)
                    if conv and i == 14:
                        qk_lo(3 * n + 1, 0, 2 * n)
                    if attn and i in (5, 9, 13, 17):
                        gi = (i - 5) // 4
                        hd, r = gi // 2, gi % 2
                        R = D * hd
                        Hb = H[pa(n, p)]
                        dve.wait_ge(S["ht_done"], 4 * k + gi + 1)
                        v.scalar_tensor_tensor(hbuf[R:R + D, 1, :], psV[R:R + D, :], 2.0 ** -PROB_BITS,
                                               hbuf[R:R + D, 0, :], ALU.mult, ALU.add).then_inc(S["hs_done"], 1)
                        dve.wait_ge(S["hh_done"], 4 * k + gi + 1)
                        v.tensor_tensor(Hb[R:R + D, 1, ba(n, b), r, 1:1 + HALF], hbuf[R:R + D, 1, :],
                                        Hb[R:R + D, 0, ba(n, b), r, 1:1 + HALF], ALU.subtract).then_inc(S["hl_done"], 1)

            dve.wait_ge(S["par_in"], 96)
            ch = Chain(dve, "c_b", 0, 6)
            ch.done(v.tensor_reduce(am[:, 4:5], par[:, 0, :], X, ALU.max, apply_absolute_value=True))
            ch.step(v.tensor_reduce(am[:, 5:6], par[:, 1, :], X, ALU.max, apply_absolute_value=True))
            v.tensor_scalar(am[:, 1:2], am[:, 4:5], (8.0 * T) ** 0.5, am[:, 5:6], ALU.mult, ALU.add) \
                .then_inc(S["bam_done"], 1)
            dve.wait_ge(S["bar_done"], 1)
            pow2(ch, amr[:, 1:2], UK, usc[:, 0:1], usc[:, 1:2])
            ch.end()
            layer_norm(0)
            weights(0)
            group_norm(0)
            step(0, 0, 0, False, True, True)
            with dve.Fori(1, NB) as n:
                step(n, 0, n, True, True, False)
            for m in range(3, 6):
                weights(m)
            step(NB, 1, 0, True, True, False)
            with dve.Fori(NB + 1, STEPS) as n:
                step(n, 1, n - NB, True, True, False)
            step(STEPS, 2, 0, True, False, False)

            ch = Chain(dve, "c_p", 0, 4)
            dve.wait_ge(S["pw_in"], 32)
            v.tensor_reduce(am[:, 3:4], pws, X, ALU.max, apply_absolute_value=True).then_inc(S["pwam_done"], 1)
            dve.wait_ge(S["pwar_done"], 1)
            pow2(ch, amr[:, 3:4], PK, pwsc[:, 0:1], pwsc[:, 1:2])
            v.tensor_scalar(alpha[:, :], vsc[:, :], pwsc[:, 1:2], None, ALU.mult).then_inc(S["pwsc_done"], 1)
            ch.end()
            dve.wait_ge(S["pwhi_done"], 1)
            v.scalar_tensor_tensor(pw[:, 1].rearrange("p a k o -> p (a k o)"), pws, pwsc[:, 0:1],
                                   pw[:, 0].rearrange("p a k o -> p (a k o)"), ALU.mult, ALU.subtract) \
                .then_inc(S["pw_done"], 1)

            def base_z(b):
                dve.wait_ge(S[f"xf_in{b % 2}"], 16 * (b // 2 + 1))
                for i in range(8):
                    v.tensor_scalar(base[:, b % 2, i, :], xf[:, b % 2, i, :], ln[:, b, i, 0:1], ln[:, b, i, 1:2],
                                    ALU.subtract, ALU.mult).then_inc(S["zf_done"], 1)

            LF = 61
            base_z(0)
            for b in range(NB):
                if b + 1 < NB:
                    base_z(b + 1)
                ch = Chain(dve, "c_f", b, LF)
                dve.wait_ge(S["base_done"], b + 1)
                if b >= 1:
                    dve.wait_ge(S["o_sum"], b)
                for i in range(8):
                    dve.wait_ge(S["pj_done"], 8 * b + i + 1)
                    ch.step(v.scalar_tensor_tensor(x1[:, i, :], pj[i][:, 0:C], alpha[:, b:b + 1], base[:, b % 2, i, :],
                                                   ALU.mult, ALU.add))
                    v.scalar_tensor_tensor(x1[:, i, :], pj[i][:, C:2 * C], alpha[:, NB + b:NB + b + 1], x1[:, i, :],
                                           ALU.mult, ALU.add).then_inc(S["pj_used"], 1)
                dve.wait_ge(S["pj_used"], 8 * (b + 1))
                stats = ln[:, b]
                layer_norm_stats(ch, x1, stats)
                rstd(ch, dve, stats[:, :, 1], 1e-5, stats[:, :, 1], "f_var", "f_sq", b + 1)
                for i in range(8):
                    v.tensor_scalar(zz[:, i, :], x1[:, i, :], stats[:, i, 0:1], stats[:, i, 1:2], ALU.subtract,
                                    ALU.mult).then_inc(S["zz_done"], 1)
                dve.wait_ge(S["zz_done"], 8 * (b + 1))
                score = tail[:, 0:3, :]
                for w, off in enumerate((32, 40, 48)):
                    ch.step(v.scalar_tensor_tensor(hot, zz[:, :, off:off + 16], 0.5,
                                                   ramp[:, 0:1, :].to_broadcast([P, 8, 16]), ALU.is_gt, ALU.mult))
                    ch.step(v.tensor_reduce(tail[:, w, :], hot, X, ALU.max))
                ch.step(v.tensor_scalar(tail[:, 3:6, :], score, -1.0, 16.0, ALU.mult, ALU.add))
                ch.step(v.scalar_tensor_tensor(tail[:, 3:6, :], score, 0.5, tail[:, 3:6, :], ALU.is_gt, ALU.mult))
                lo, hi, sa = tail[:, 3, :], tail[:, 4, :], tail[:, 5, :]
                ch.done(v.scalar_tensor_tensor(taili[:, 0, :], hi, 16.0, lo, ALU.mult, ALU.add))
                ch.step(v.tensor_copy(taili[:, 1, :], sa))
                ch.done(v.tensor_tensor(taili[:, 2, :], taili[:, 0, :], taili[:, 1, :], ALU.logical_shift_left))
                ch.step(v.tensor_tensor(taili[:, 3, :], taili[:, 0, :], taili[:, 1, :], ALU.logical_shift_right))
                ch.step(v.tensor_scalar(taili[:, 2, :], taili[:, 2, :], 255, None, ALU.bitwise_and))
                mark, shl, shr, a1, a2 = (tail[:, 6 + q, :] for q in range(5))
                for q, ch_ in ((mark, 0), (shl, 39), (shr, 40)):
                    ch.done(v.tensor_scalar(q, zz[:, :, ch_], 0.5, None, ALU.is_gt))
                ch.wait()
                ch.step(v.tensor_tensor(a1, mark, shl, ALU.mult))
                ch.step(v.tensor_tensor(mark, mark, a1, ALU.subtract))
                ch.step(v.tensor_tensor(a2, mark, shr, ALU.mult))
                ch.done(v.tensor_tensor(shl, taili[:, 2, :], a1, ALU.mult))
                ch.step(v.tensor_tensor(shr, taili[:, 3, :], a2, ALU.mult))
                ch.done(v.tensor_tensor(taili[:, 4, :], shl, shr, ALU.add))
                ch.step(v.tensor_tensor(a1, a1, a2, ALU.add))
                ch.done(v.tensor_scalar(taili[:, 5, :], taili[:, 4, :], 15, None, ALU.bitwise_and))
                ch.step(v.tensor_scalar(taili[:, 6, :], taili[:, 4, :], 4, None, ALU.logical_shift_right))
                for q in range(2):
                    ch.step(v.scalar_tensor_tensor(tail[:, 11 + q, :], taili[:, 5 + q, :], 1.0, a1, ALU.add, ALU.mult))
                    ch.step(v.tensor_scalar(tail[:, 11 + q, :], tail[:, 11 + q, :], -1.0, None, ALU.add))
                dve.wait_ge(S["o_sum"], b + 1)
                for q, off in enumerate((64, 72)):
                    ch.step(v.tensor_tensor(hot, ramp[:, 1:2, :].to_broadcast([P, 8, 16]),
                                            tail[:, 11 + q, :].rearrange("p (i o) -> p i o", o=1)
                                            .to_broadcast([P, 8, 16]), ALU.is_equal))
                    w = ob[:, b % 2, :, off:off + 16]
                    last = v.scalar_tensor_tensor(w, hot, 2.0, w, ALU.mult, ALU.add)
                    if q == 0:
                        ch.step(last)
                    else:
                        last.then_inc(S["o_done"], 1)
                ch.end()


def kernel(x, L0_conv_gn_gamma, L0_conv_gn_beta, L0_conv_qkv_w, L0_conv_qkv_b, L0_conv_proj_w, L0_conv_proj_b):
    import numpy as np
    import concourse.bacc as bacc
    from concourse.bass_utils import run_bass_kernel_spmd

    order = []
    for p in range(PAIRS):
        heads = (2 * p, 2 * p + 1)
        order += [3 * D * h + 2 * D + c for h in heads for c in range(D)]
        order += [3 * D * h + c for h in heads for c in range(2 * D)]
    order = np.array(order)
    x, wq, wp = np.asarray(x), np.asarray(L0_conv_qkv_w), np.asarray(L0_conv_proj_w)
    w = wq[order].reshape(6, P, CT, P, PH_TAPS, 2).transpose(0, 2, 3, 5, 4, 1).reshape(6, CT, P, TAPS * P)
    ident = np.eye(P, dtype=np.float32)
    group = np.kron(np.eye(P // 8, dtype=np.float32), np.full((8, 8), 0.125, np.float32))
    ramp = np.tile(np.concatenate([16 - np.arange(16), np.arange(16)]).astype(np.float32), (P, 1))
    data = {
        "x_tok": x.reshape(NB, C, T).transpose(0, 2, 1),
        "w_qkv": w,
        "b_qkv": np.asarray(L0_conv_qkv_b)[order].reshape(6, P).T,
        "gamma": np.asarray(L0_conv_gn_gamma).reshape(CT, P).T,
        "beta": np.asarray(L0_conv_gn_beta).reshape(CT, P).T,
        "w_proj": wp.reshape(C, PAIRS, P, PTAPS).transpose(2, 1, 3, 0).reshape(P, PAIRS * PTAPS * C),
        "b_proj": np.asarray(L0_conv_proj_b).reshape(1, C),
        "ident": ident, "group": group, "ramp": ramp,
    }
    nc = bacc.Bacc("TRN2", target_bir_lowering=False, num_devices=1)
    arrays, args = {}, []
    for name, a in data.items():
        arrays[name] = np.ascontiguousarray(a)
        args.append(nc.dram_tensor(name, a.shape, mybir.dt.from_np(a.dtype), kind="ExternalInput").ap())
    args.append(nc.dram_tensor("out_tok", (NB, T, C), F32, kind="ExternalOutput").ap())
    build(nc, *args)
    r = run_bass_kernel_spmd(nc, [arrays], core_ids=[0])
    out = np.asarray(r.results[0]["out_tok"])
    return np.ascontiguousarray(out.transpose(0, 2, 1)).reshape(NB, C, 32, 32)
```

```python
from contextlib import ExitStack

import concourse.bass as bass
from concourse import mybir

F32 = mybir.dt.float32
F16 = mybir.dt.float16
I32 = mybir.dt.int32
ALU = mybir.AluOpType
ACT = mybir.ActivationFunctionType
X = mybir.AxisListType.X
ABSMAX = bass.bass_isa.ReduceOp.absmax

P = 128
NB, T, C = 4, 1024, 256
CT = C // P
HALF = T // 2
TAPS, PTAPS = 16, 5
PH_TAPS = TAPS // 2
SUM_TAPS = 2
SUMS = CT * PH_TAPS // SUM_TAPS
PARTS = SUMS + 4
PAIRS, TILES = 2, 3
STEPS = PAIRS * NB
D = 64
UNITS = 16
SLOTS = 18
SEQW = HALF + PH_TAPS
HW = HALF + 2
LEFT = 4
EXP23 = float(1 << 23)
PROB_BITS = 13
WK, UK, QK, PK = 13, 13, 14, 14


def build(nc, x_tok, w_qkv, b_qkv, gamma, beta, w_proj, b_proj, ident_in, group_in, ramp_in, out_tok):
    with ExitStack() as ctx:
        def sb(name, shape, dt):
            return ctx.enter_context(nc.sbuf_tensor(name, shape, dt))

        def ps(name, shape):
            return ctx.enter_context(nc.psum_tensor(name, shape, F32))

        def sem(name):
            return ctx.enter_context(nc.semaphore(name))

        W = sb("W", [P, TILES, 2, CT, 3, PH_TAPS, P], F16)
        U = sb("U", [P, 2, CT, NB, 3, SEQW], F16)
        stack = sb("stack", [P, 2, 3, T], F16)
        yv = sb("yv", [P, T], F32)
        yqk = sb("yqk", [P, T], F32)
        m_sb = sb("m_sb", [P, HALF], F32)
        arena = sb("arena", [P, 5 * T], F32)
        prob = arena[:, 0:T]
        probT = arena[:, T:5 * T].bitcast(F16).rearrange("p (l s t) -> p l s t", l=2, s=8)
        eo = arena[:, 0:CT * 2 * SEQW].rearrange("p (c r w) -> p c r w", c=CT, r=2)
        diff = arena[:, CT * 2 * SEQW:2 * CT * 2 * SEQW].rearrange("p (d c w) -> p d c w", d=2, c=CT)
        vT = sb("vT", [P, 8, 2, P], F16)
        hbuf = sb("hbuf", [P, 2, HALF], F32)
        wsum = sb("wsum", [P, 2, SUM_TAPS, P], F32)
        H = [sb(f"H{p}", [P, 2, NB, 2, HW], F16) for p in range(PAIRS)]
        xs = H[0][:, :, :, :, :].rearrange("p a b r w -> p (a b r w)")[:, 0:8192].bitcast(F32) \
            .rearrange("p (n i c) -> p n i c", n=2, i=8)
        wst = H[1][:, :, :, :, :].rearrange("p a b r w -> p (a b r w)")[:, 0:8192].bitcast(F32) \
            .rearrange("p (c s k o) -> p c s k o", c=CT, s=2, k=PH_TAPS)
        ident = sb("ident_sb", [P, P], F32)
        group = sb("group_sb", [P, P], F32)
        ln = sb("ln", [P, NB, 8, 2], F32)
        st = sb("st", [P, 8, 6], F32)
        gs = sb("gs", [P, CT, 4], F32)
        gn = sb("gn", [P, CT, 4], F32)
        ab = sb("ab", [P, CT, 2], F32)
        nt = sb("nt", [P, 3, 8], F32)
        par = sb("par", [P, 2, CT], F32)
        qb = sb("qb", [P, 6], F32)
        am = sb("am", [P, 8], F32)
        amr = sb("amr", [P, 8], F32)
        bits = sb("bits", [P, 2], I32)
        usc = sb("usc", [P, 2], F32)
        wsc = sb("wsc", [P, 2, 6], F32)
        isc = sb("isc", [P, 6], F32)
        ysc = sb("ysc", [P, 2], F32)
        vsc = sb("vsc", [P, STEPS], F32)
        vscale = sb("vscale", [P, 1], F32)
        esc = sb("esc", [P, 2, 2], F32)
        smx = sb("smx", [P, 4], F32)
        Wf = W[:, :, :, :, :, :, :].rearrange("p a b c d e f -> p (a b c d e f)")
        Uf = U[:, :, :, :, :, :].rearrange("p a b c d e -> p (a b c d e)")
        PWN = PAIRS * PTAPS * C
        pws = Wf[:, 0:2 * PWN].bitcast(F32)
        pw = Wf[:, 2 * PWN:4 * PWN].rearrange("p (l a k o) -> p l a k o", l=2, a=PAIRS, k=PTAPS)
        x1, zz, ob = (Wf[:, 4 * PWN + q * 8192:4 * PWN + (q + 1) * 8192].bitcast(F32)
                      .rearrange("p (n i c) -> p n i c", n=2, i=8) for q in range(3))
        xf = Uf[:, 0:8192].bitcast(F32).rearrange("p (n i c) -> p n i c", n=2, i=8)
        base = Uf[:, 8192:16384].bitcast(F32).rearrange("p (n i c) -> p n i c", n=2, i=8)
        pbb = Uf[:, 16384:16896].bitcast(F32)
        hot = Uf[:, 16896:17152].bitcast(F32).rearrange("p (i k) -> p i k", i=8)
        tail = Uf[:, 17152:17152 + 512].bitcast(F32).rearrange("p (f i) -> p f i", i=8)
        taili = Uf[:, 17664:17664 + 256].bitcast(I32).rearrange("p (f i) -> p f i", i=8)
        ramp = sb("ramp_sb", [P, 2, 16], F32)
        alpha = sb("alpha", [P, STEPS], F32)
        nmr = sb("nmr", [P, NB, 8], F32)
        pwsc = sb("pwsc", [P, 2], F32)

        bank = [ps("cM", [P, HALF]), ps("cP", [P, HALF]), ps("cQ", [P, HALF])]
        psS = ps("psS", [P, T])
        psT = ps("psT", [P, T])
        psV = ps("psV", [P, HALF])

        names = """par_in pads x_in0 x_in1 z_done zT_done gstat_done gmm_done ab_done eo_done diff_done uhi_done
            ulo_done ln_sq ln_var gn_var gn_sq ws_in0 ws_in1 wam_done war_done wsc_done wsum_done whi_done wlo_done
            bam_done bar_done conv_done m_done y0_done y1_done yam_done yar_done ysc_done
            s_done nb_done e_done pn_done t_done ph_done pl_done pv_done ht_done hs_done hh_done hl_done
            vt_done vh_done vl_done qk_hi qk_done pw_in pwam_done pwar_done pwsc_done pwhi_done pw_done
            xf_in0 xf_in1 xf_used zf_done nmr_done base_done pj_done pj_used f_var f_sq f_nm o_sum zz_done o_done out_sent0 out_sent1
            c_a c_b c_g c_m c_w c_u c_y c_s c_k c_x c_f c_p c_z""".split()
        S = {n: sem(n) for n in names}

        class Chain:
            def __init__(self, eng, name, run, per_run):
                self.eng, self.sem, self.start, self.per_run, self.n = eng, S[name], run * per_run, per_run, 0

            def done(self, ins):
                ins.then_inc(self.sem, 1)
                self.n += 1

            def wait(self):
                self.eng.wait_ge(self.sem, self.start + self.n)

            def step(self, ins):
                self.done(ins)
                self.wait()

            def end(self):
                assert self.n == self.per_run, (self.sem, self.n, self.per_run)

        def pow2(ch, src, k, scale, inverse):
            v = nc.vector
            ch.step(v.tensor_scalar(inverse, src, 1e-30, None, ALU.max))
            ch.step(v.tensor_scalar(bits[:, 0:1], inverse.bitcast(I32), 0x7F800000, None, ALU.bitwise_and))
            ch.done(v.tensor_scalar(scale.bitcast(I32), bits[:, 0:1], -1.0, (254 + k) * EXP23, ALU.mult, ALU.add))
            ch.step(v.tensor_scalar(inverse.bitcast(I32), bits[:, 0:1], 1.0, -k * EXP23, ALU.mult, ALU.add))

        def rstd(ch, eng, var, eps, out, sq_asked, sq_done, runs):
            v = nc.vector
            n = nt[:, 0, 0:var.shape[-1]]
            s = nt[:, 1, 0:var.shape[-1]]
            q = nt[:, 2, 0:var.shape[-1]]
            v.tensor_scalar(n, var, eps, None, ALU.add).then_inc(S[sq_asked], 1)
            eng.wait_ge(S[sq_done], runs)
            ch.step(v.reciprocal(q, s))
            ch.step(v.tensor_tensor(s, n, q, ALU.mult))
            ch.step(v.tensor_tensor(s, s, q, ALU.mult))
            ch.step(v.tensor_scalar(s, s, -0.5, 1.5, ALU.mult, ALU.add))
            ch.step(v.tensor_tensor(out, q, s, ALU.mult))

        EXTRA = {
            "start": {0: [("ln", 0), ("wmax", 0), ("wscale", 0), ("zT", 0), ("gn", 0), ("gmm", 0), ("wsum", 0),
                          ("split", 0), ("w0", 0), ("w1", 0)]},
            0: {0: [("wmax", 1)], 1: [("wscale", 1)], 2: [("wsum", 1)], 3: [("w0", 1)], 4: [("w1", 1)],
                5: [("ln", 1)], 6: [("zT", 1)], 7: [("wmax", 2), ("gn", 1)], 8: [("wscale", 2), ("gmm", 1), ("split", 1)],
                9: [("wsum", 2)], 10: [("w0", 2), ("w1", 2)], 11: [("ln", 2)], 12: [("zT", 2)],
                13: [("gn", 2), ("ln", 3)], 14: [("gmm", 2), ("split", 2)], 15: [("zT", 3)], 16: [("gn", 3)],
                17: [("gmm", 3), ("split", 3)]},
            3: {1: [("wmax", 3)], 2: [("wscale", 3)], 3: [("wsum", 3)], 5: [("w0", 3)], 7: [("w1", 3)],
                10: [("wmax", 4)], 11: [("wscale", 4)], 12: [("wsum", 4)], 14: [("w0", 4)], 15: [("w1", 4)]},
            4: {3: [("wmax", 5)], 4: [("wscale", 5)], 5: [("wsum", 5)], 6: [("w0", 5)], 7: [("w1", 5)],
                8: [("pads", 0)]},
        }
        LATE = {}

        def late(slot, kind, b, i=0):
            LATE.setdefault(slot, []).append((kind, b, i))

        late(0, "nmr", 0)
        late(1, "pw", 0)
        for b in range(NB):
            for i in range(8):
                q = 8 * b + i
                if i == 0:
                    late(2 + 5 * b, "base", b)
                late(3 + q * 15 // 24 if b < 3 else 18 + i // 2, "tile", b, i)
        for b in range(NB):
            for n, kind in enumerate(("stats", "norm", "sum", "find", "shift", "mark")):
                late(8 + 5 * b + n, kind, b)
        LAST = max(LATE) + 1

        def is_int(v):
            return isinstance(v, int)

        def wait(eng, name, value):
            if not (is_int(value) and value <= 0):
                eng.wait_ge(S[name], value)

        def pa(n, p):
            return p - 1 if is_int(n) and n % NB == 0 else p

        def ba(n, b):
            return (n - 1) % NB if is_int(n) else b - 1

        block = ctx.enter_context(nc.Block())

        @block.sync
        def _(sp):
            xv = x_tok.rearrange("b (j p r) c -> b p j (r c)", j=4, r=2)
            ov = out_tok.rearrange("b (j p r) c -> b p j (r c)", j=4, r=2)

            def load_x(b):
                if b >= 2:
                    sp.wait_ge(S["zT_done"], b - 1)
                sp.dma_start(xs[:, b % 2, :, :].rearrange("p (j r) c -> p j (r c)", r=2), xv[b]) \
                    .then_inc(S[f"x_in{b % 2}"], 16)

            def load_w(m):
                if m >= 1:
                    sp.wait_ge(S["wlo_done"], PARTS * m)
                for c in range(CT):
                    sp.dma_start(wst[:, c].rearrange("p s k o -> p (s k o)"), w_qkv[m, c]).then_inc(S[f"ws_in{c}"], 16)

            load_x(0)
            for dst, src in ((par[:, 0, :], gamma), (par[:, 1, :], beta), (qb[:, :], b_qkv), (ident[:, :], ident_in),
                             (group[:, :], group_in), (ramp[:, :, :].rearrange("p a b -> p (a b)"), ramp_in)):
                sp.dma_start(dst, src).then_inc(S["par_in"], 16)
            load_w(0)
            load_x(1)
            load_w(1)
            load_x(2)
            load_w(2)
            load_x(3)
            for m in range(3, 6):
                load_w(m)
            sp.wait_ge(S["conv_done"], 9 * STEPS)
            sp.dma_start(pws, w_proj).then_inc(S["pw_in"], 16)
            sp.dma_start(pbb, b_proj.to_broadcast([P, C])).then_inc(S["pw_in"], 16)
            for b in range(NB):
                if b >= 2:
                    sp.wait_ge(S["base_done"], b - 1)
                sp.dma_start(xf[:, b % 2, :, :].rearrange("p (j r) c -> p j (r c)", r=2), xv[b]) \
                    .then_inc(S[f"xf_in{b % 2}"], 16)
            for b in range(NB):
                sp.wait_ge(S["o_done"], b + 1)
                sp.dma_start(ov[b], ob[:, b % 2, :, :].rearrange("p (j r) c -> p j (r c)", r=2)) \
                    .then_inc(S[f"out_sent{b % 2}"], 16)
            sp.wait_ge(S["out_sent0"], 32)
            sp.wait_ge(S["out_sent1"], 32)

        @block.gpsimd
        def _(pool):
            g = nc.gpsimd

            def extra(kind, k):
                if kind == "wscale":
                    pool.wait_ge(S["wam_done"], k + 1)
                    g.partition_all_reduce(amr[:, 0:1], am[:, 0:1], P, ABSMAX).then_inc(S["war_done"], 1)
                if kind == "wsum":
                    for h in range(SUMS):
                        c, t = h // (SUMS // CT), h % (SUMS // CT) * SUM_TAPS
                        wait(pool, "wlo_done", PARTS * k + h - 1 if h >= 2 else PARTS * (k - 1) + SUMS)
                        pool.wait_ge(S[f"ws_in{c}"], 16 * (k + 1))
                        g.tensor_tensor(wsum[:, h % 2], wst[:, c, 0, t:t + SUM_TAPS], wst[:, c, 1, t:t + SUM_TAPS],
                                        ALU.add).then_inc(S["wsum_done"], 1)
                if kind == "split":
                    pool.wait_ge(S["eo_done"], 4 * (k + 1))
                    wait(pool, "ulo_done", 3 * k)
                    for d in range(2):
                        g.tensor_tensor(diff[:, d, :, 0:SEQW - 1], eo[:, :, 1, d:d + SEQW - 1], eo[:, :, 0, 1:SEQW],
                                        ALU.subtract).then_inc(S["diff_done"], 1)
                if kind == "pads":
                    pool.wait_ge(S["wlo_done"], 6 * PARTS)
                    for p in range(PAIRS):
                        for e in (0, HW - 1):
                            g.memset(H[p][:, :, :, :, e:e + 1].rearrange("p a b r w -> p (a b r) w"), 0.0) \
                                .then_inc(S["pads"], 1)

            def amax(run):
                pool.wait_ge(S["yam_done"], run + 1)
                g.tensor_tensor(am[:, 6:7], am[:, 2:3], ramp[:, 1, 1:2], ALU.mult)
                pool.drain()
                g.partition_all_reduce(amr[:, 2:3], am[:, 6:7], P, ABSMAX).then_inc(S["yar_done"], 1)

            pool.wait_ge(S["bam_done"], 1)
            g.partition_all_reduce(amr[:, 1:2], am[:, 1:2], P, ABSMAX).then_inc(S["bar_done"], 1)
            g.memset(eo[:, :, :, 0:LEFT], 0.0).then_inc(S["pads"], 1)
            g.memset(eo[:, :, :, LEFT + HALF:SEQW], 0.0).then_inc(S["pads"], 1)
            for kind, k in EXTRA["start"][0]:
                extra(kind, k)

            def step(n, attn, more=None):
                for i in range(SLOTS):
                    for kind, k in EXTRA.get(more, {}).get(i, []):
                        extra(kind, k)
                    if attn and i == 0:
                        amax(3 * n - 1)
                    if i == 6:
                        amax(3 * n)
                    if i == 12:
                        amax(3 * n + 1)

            step(0, False, 0)
            with pool.Fori(1, NB - 1) as n:
                step(n, True)
            step(NB - 1, True, NB - 1)
            step(NB, True, NB)
            with pool.Fori(NB + 1, STEPS) as n:
                step(n, True)
            amax(3 * STEPS - 1)
            for i in range(LAST):
                for kind, b, _ in LATE.get(i, []):
                    if kind == "pw":
                        pool.wait_ge(S["pwam_done"], 1)
                        g.partition_all_reduce(amr[:, 3:4], am[:, 3:4], P, ABSMAX).then_inc(S["pwar_done"], 1)
                    if kind == "base":
                        pool.wait_ge(S["pw_in"], 32)
                        pool.wait_ge(S["zf_done"], 8 * (b + 1))
                        g.tensor_tensor(base[:, b % 2], base[:, b % 2], xf[:, b % 2], ALU.add).then_inc(S["c_z"], 1)
                        pool.wait_ge(S["c_z"], b + 1)
                        g.tensor_tensor(base[:, b % 2], base[:, b % 2], pbb[:, :].rearrange("p (o c) -> p o c", o=1)
                                        .to_broadcast([P, 8, C]), ALU.add).then_inc(S["base_done"], 1)
                    if kind == "sum":
                        pool.wait_ge(S["zz_done"], 8 * (b + 1))
                        if b >= 2:
                            pool.wait_ge(S[f"out_sent{b % 2}"], 16)
                        g.tensor_tensor(ob[:, b % 2], x1[:, b % 2], zz[:, b % 2], ALU.add).then_inc(S["o_sum"], 1)

        @block.scalar
        def _(act):
            a = nc.scalar.activation

            def sqrt(asked, done, runs, width):
                act.wait_ge(S[asked], runs)
                a(nt[:, 1, 0:width], nt[:, 0, 0:width], ACT.Sqrt).then_inc(S[done], 1)

            def extra(kind, k):
                j = k % 3
                if kind == "ln":
                    sqrt("ln_var", "ln_sq", k + 1, 8)
                if kind == "gn":
                    sqrt("gn_var", "gn_sq", k + 1, CT)
                    act.wait_ge(S["ab_done"], k + 1)
                    act.wait_ge(S["pads"], 2)
                    wait(act, "ulo_done", 3 * k)
                    wait(act, "diff_done", 2 * k)
                    for c, src in ((0, psS), (1, psT)):
                        for r in range(2):
                            a(eo[:, c, r, LEFT:LEFT + HALF], src[:, r * HALF:(r + 1) * HALF], ACT.Identity,
                              bias=ab[:, c, 1:2], scale=ab[:, c, 0:1]).then_inc(S["eo_done"], 1)
                if kind == "split":
                    act.wait_ge(S["eo_done"], 4 * (k + 1))
                    a(U[:, 0, :, k, 0, 0:SEQW - 1], eo[:, :, 0, 1:SEQW], ACT.Copy).then_inc(S["uhi_done"], 1)
                    for d in range(2):
                        act.wait_ge(S["diff_done"], 2 * k + d + 1)
                        a(U[:, 0, :, k, 1 + d, 0:SEQW - 1], diff[:, d, :, 0:SEQW - 1], ACT.Copy) \
                            .then_inc(S["uhi_done"], 1)
                if kind in ("wsum", "w0", "w1"):
                    act.wait_ge(S["wsc_done"], k + 1)
                    if k >= 3:
                        act.wait_ge(S["conv_done"], 27 + 3 * j + 1 + ("wsum", "w0", "w1").index(kind))
                scale = wsc[:, 0, k:k + 1]
                if kind == "wsum":
                    for h in range(SUMS):
                        act.wait_ge(S["wsum_done"], SUMS * k + h + 1)
                        c, t = h // (SUMS // CT), h % (SUMS // CT) * SUM_TAPS
                        a(W[:, j, 0, c, 0, t:t + SUM_TAPS], wsum[:, h % 2], ACT.Copy, scale=scale) \
                            .then_inc(S["whi_done"], 1)
                if kind in ("w0", "w1"):
                    q = int(kind[1])
                    for c in range(CT):
                        a(W[:, j, 0, c, 1 + q], wst[:, c, q], ACT.Copy, scale=scale).then_inc(S["whi_done"], 1)

            def qk_hi(run, hd):
                act.wait_ge(S["ysc_done"], run + 1)
                a(stack[0:D, hd, 0, :], yqk[0:D, :], ACT.Copy, scale=ysc[0:D, 0:1]).then_inc(S["qk_hi"], 1)
                a(stack[D:P, hd, 1, :], yqk[D:P, :], ACT.Copy, scale=ysc[D:P, 0:1]).then_inc(S["qk_hi"], 1)

            def last_stage(kind, b):
                if kind == "pw":
                    act.wait_ge(S["pwsc_done"], 1)
                    a(pw[:, 0].rearrange("p a k o -> p (a k o)"), pws, ACT.Copy, scale=pwsc[:, 0:1]) \
                        .then_inc(S["pwhi_done"], 1)
                if kind == "base":
                    act.wait_ge(S["nmr_done"], 1)
                    act.wait_ge(S[f"xf_in{b % 2}"], 16 * (b // 2 + 1))
                    if b >= 2:
                        act.wait_ge(S["pj_used"], 8 * (b - 1))
                    for i in range(8):
                        a(base[:, b % 2, i, :], xf[:, b % 2, i, :], ACT.Identity, bias=nmr[:, b, i:i + 1],
                          scale=ln[:, b, i, 1:2]).then_inc(S["zf_done"], 1)
                if kind == "norm":
                    sqrt("f_var", "f_sq", b + 1, 8)
                    act.wait_ge(S["f_nm"], b + 1)
                    wait(act, "o_done", b - 1)
                    for i in range(8):
                        a(zz[:, b % 2, i, :], x1[:, b % 2, i, :], ACT.Identity, bias=nmr[:, b, i:i + 1],
                          scale=ln[:, b, i, 1:2]).then_inc(S["zz_done"], 1)

            def step(n, p, b, attn, conv, more=None):
                k = n - 1
                for i in range(SLOTS if conv else LAST):
                    for kind, e in EXTRA.get(more, {}).get(i, []):
                        extra(kind, e)
                    if attn and i == 0:
                        act.wait_ge(S["vt_done"], k + 1)
                        act.wait_ge(S["ysc_done"], 3 * k + 1)
                        vt = psT[:, :].rearrange("p (s h c) -> p s h c", s=8, h=2)
                        a(vT[:, :, 0, 0:D], vt[:, :, 0, :], ACT.Copy, scale=vscale[:, 0:1]).then_inc(S["vh_done"], 1)
                        a(vT[:, :, 1, D:P], vt[:, :, 1, :], ACT.Copy, scale=vscale[:, 0:1]).then_inc(S["vh_done"], 1)
                    if attn and 1 <= i <= UNITS:
                        u = i - 1
                        act.wait_ge(S["t_done"], 16 * k + u + 1)
                        if u >= 4:
                            act.wait_ge(S["pv_done"], 4 * k + u // 4)
                        a(probT[:, 0, :, u % 4 * P:(u % 4 + 1) * P], psT[:, :].rearrange("p (s t) -> p s t", s=8),
                          ACT.Copy).then_inc(S["ph_done"], 1)
                    if attn and i < UNITS:
                        u, hd = i, i // 8
                        act.wait_ge(S["nb_done"], 16 * k + u + 1)
                        if u:
                            act.wait_ge(S["t_done"], 16 * k + u)
                        a(prob, psS[:, :], ACT.Exp, bias=smx[:, 1:2], scale=esc[:, hd, 0:1],
                          accum_out=smx[:, 2:3]).then_inc(S["e_done"], 1)
                    if conv and i in (2, 8, 14):
                        j = i // 6
                        act.wait_ge(S["conv_done"], 9 * n + 3 * j + 1)
                        wait(act, "y1_done", 3 * n + j)
                        a(m_sb[:, :], bank[0][:, :], ACT.Identity, bias=qb[:, 3 * p + j:3 * p + j + 1],
                          scale=isc[:, 3 * p + j:3 * p + j + 1]).then_inc(S["m_done"], 1)
                    if attn and i == 1:
                        qk_hi(3 * k + 2, 1)
                    if conv and i == 13:
                        qk_hi(3 * n + 1, 0)
                    if attn and i in (5, 9, 13, 17):
                        gi = (i - 5) // 4
                        hd, r = gi // 2, gi % 2
                        R, O = D * hd, D * (1 - hd)
                        act.wait_ge(S["pv_done"], 4 * k + gi + 1)
                        a(hbuf[R:R + D, 0, :], psV[O:O + D, :], ACT.Copy, scale=2.0 ** -PROB_BITS) \
                            .then_inc(S["ht_done"], 1)
                        act.wait_ge(S["hs_done"], 4 * k + gi + 1)
                        a(H[pa(n, p)][R:R + D, 0, ba(n, b), r, 1:1 + HALF], hbuf[R:R + D, 1, :], ACT.Copy) \
                            .then_inc(S["hh_done"], 1)
                    if not conv:
                        for kind, e, _ in LATE.get(i, []):
                            last_stage(kind, e)

            for kind, e in EXTRA["start"][0]:
                extra(kind, e)
            step(0, 0, 0, False, True, 0)
            with act.Fori(1, NB - 1) as n:
                step(n, 0, n, True, True)
            step(NB - 1, 0, NB - 1, True, True, NB - 1)
            step(NB, 1, 0, True, True, NB)
            with act.Fori(NB + 1, STEPS) as n:
                step(n, 1, n - NB, True, True)
            step(STEPS, 2, 0, True, False)

        @block.tensor
        def _(pe):
            mm, tr = nc.tensor.matmul, nc.tensor.transpose

            batch_reg = pe.alloc_register("batch")

            def fresh(b):
                if is_int(b):
                    return b
                pe.reg_mov(batch_reg, b)
                return pe.snap(batch_reg)

            def z_transpose(b):
                pe.wait_ge(S["z_done"], 8 * (b + 1))
                wait(pe, "eo_done", 4 * b)
                for i in range(8):
                    j, r = i // 2, i % 2
                    for c, dst in ((0, psS), (1, psT)):
                        last = tr(dst[:, r * HALF + j * P:r * HALF + (j + 1) * P], xs[:, b % 2, i, c * P:(c + 1) * P],
                                  ident[:, :])
                last.then_inc(S["zT_done"], 1)

            def group_mean(b):
                pe.wait_ge(S["gstat_done"], b + 1)
                mm(psV[:, 0:2 * CT], group[:, :], gs[:, :, 0:2].rearrange("p c k -> p k c"), start=True, stop=True) \
                    .then_inc(S["gmm_done"], 1)

            def project(b, i):
                q, (j, r) = 8 * b + i, (i // 2, i % 2)
                if i == 0:
                    pe.wait_ge(S["hl_done"], 4 * (NB + b + 1))
                if q == 0:
                    pe.wait_ge(S["pw_done"], 1)
                    pe.wait_ge(S["pads"], 6)
                if q < 3:
                    pe.wait_ge(S[("m_done", "y0_done", "y1_done")[q]], 3 * STEPS)
                else:
                    pe.wait_ge(S["pj_used"], q - 2)
                for p in range(PAIRS):
                    for t in range(PTAPS):
                        d = r + t - 2
                        col = 1 + d // 2 + j * P
                        for hl, wl in ((0, 0), (0, 1), (1, 0)):
                            last = mm(bank[q % 3][:, p * C:(p + 1) * C], H[p][:, hl, b, d % 2, col:col + P],
                                      pw[:, wl, p, t, :], start=(t == 0 and hl + wl == 0),
                                      stop=(t == PTAPS - 1 and hl == 1), skip_group_check=True)
                last.then_inc(S["pj_done"], 1)

            def step(n, p, b, attn, conv, more=None):
                k = n - 1
                for i in range(SLOTS if conv else LAST):
                    for kind, e in EXTRA.get(more, {}).get(i, []):
                        if kind == "zT":
                            z_transpose(e)
                        if kind == "gmm":
                            group_mean(e)
                    if attn and i in (5, 9, 13, 17):
                        gi = (i - 5) // 4
                        hd = gi // 2
                        pe.wait_ge(S["pl_done"], 16 * k + 4 * gi + 4)
                        if gi == 0:
                            pe.wait_ge(S["vl_done"], 2 * k + 2)
                        if gi:
                            pe.wait_ge(S["hs_done"], 4 * k + gi)
                        for s in range(8):
                            for l in range(2):
                                last = mm(psV[:, :], vT[:, s, hd, :], probT[:, l, s, :], start=(s + l == 0),
                                          stop=(s + l == 8))
                        last.then_inc(S["pv_done"], 1)
                    if attn and 1 <= i <= UNITS:
                        u = i - 1
                        pe.wait_ge(S["pn_done"], 16 * k + u + 1)
                        if u == 0:
                            pe.wait_ge(S["vl_done"], 2 * k + 2)
                        else:
                            pe.wait_ge(S["pl_done"], 16 * k + u)
                        for s in range(8):
                            last = tr(psT[:, s * P:(s + 1) * P], prob[:, s * P:(s + 1) * P], ident[:, :])
                        last.then_inc(S["t_done"], 1)
                    if attn and i < UNITS:
                        u, hd = i, i // 8
                        if u % 8 == 0:
                            pe.wait_ge(S["qk_done"], 2 * k + hd + 1)
                        if u:
                            pe.wait_ge(S["e_done"], 16 * k + u)
                        for h in range(2):
                            for l in range(2):
                                last = mm(psS[:, h * HALF:(h + 1) * HALF], stack[:, hd, 0, u % 8 * P:(u % 8 + 1) * P],
                                          stack[:, hd, 1 + l, h * HALF:(h + 1) * HALF], start=(l == 0), stop=(l == 1))
                        last.then_inc(S["s_done"], 1)
                    if conv:
                        q = i // 2
                        j, kind = q // 3, q % 3
                        if i % 2 == 0:
                            wait(pe, ("m_done", "y0_done", "y1_done")[kind], 3 * n + j)
                            pe.wait_ge(S["wlo_done"], PARTS * (3 * p + j) + SUMS + 2 * kind)
                            if i == 0 or more == 0 and i <= 4:
                                pe.wait_ge(S["ulo_done"], kind + 1 if more == 0 else 3 * NB)
                        c = i % 2
                        bb = fresh(b)
                        for t in range(PH_TAPS):
                            for wl, ul in ((0, 0), (0, 1), (1, 0)):
                                last = mm(bank[kind][:, :], W[:, j, wl, c, kind, t, :], U[:, ul, c, bb, kind, t:t + HALF],
                                          start=(c == 0 and t == 0 and wl + ul == 0),
                                          stop=(c == 1 and t == PH_TAPS - 1 and wl == 1))
                        if i % 2 == 1:
                            last.then_inc(S["conv_done"], 1)
                    if not conv:
                        for kind, e, t in LATE.get(i, []):
                            if kind == "tile":
                                project(e, t)
                if conv:
                    pe.wait_ge(S["y1_done"], 3 * n + 1)
                    if attn:
                        pe.wait_ge(S["pl_done"], 16 * n)
                    else:
                        pe.wait_ge(S["eo_done"], 4 * NB)
                    for s in range(8):
                        last = tr(psT[:, s * P:(s + 1) * P], yv[:, s * P:(s + 1) * P], ident[:, :])
                    last.then_inc(S["vt_done"], 1)

            pe.wait_ge(S["par_in"], 96)
            z_transpose(0)
            group_mean(0)
            step(0, 0, 0, False, True, 0)
            with pe.Fori(1, NB - 1) as n:
                step(n, 0, n, True, True)
            step(NB - 1, 0, NB - 1, True, True)
            step(NB, 1, 0, True, True)
            with pe.Fori(NB + 1, STEPS) as n:
                step(n, 1, n - NB, True, True)
            step(STEPS, 2, 0, True, False)

        @block.vector
        def _(dve):
            v = nc.vector

            def layer_norm_stats(ch, src, dst):
                for i in range(8):
                    ch.done(v.bn_stats(st[:, i, :], src[:, i, :]))
                ch.wait()
                for i in range(8):
                    ch.done(v.bn_aggr(dst[:, i, :], st[:, i, :]))
                ch.wait()

            def layer_norm(b):
                ch = Chain(dve, "c_a", b, 21)
                dve.wait_ge(S[f"x_in{b % 2}"], 16 * (b // 2 + 1))
                layer_norm_stats(ch, xs[:, b % 2], ln[:, b])
                rstd(ch, dve, ln[:, b, :, 1], 1e-6, ln[:, b, :, 1], "ln_var", "ln_sq", b + 1)
                ch.end()
                for i in range(8):
                    v.tensor_scalar(xs[:, b % 2, i, :], xs[:, b % 2, i, :], ln[:, b, i, 0:1], ln[:, b, i, 1:2],
                                    ALU.subtract, ALU.mult).then_inc(S["z_done"], 1)

            def group_norm(b):
                ch = Chain(dve, "c_g", b, 19)
                dve.wait_ge(S["zT_done"], b + 1)
                for c, src in ((0, psS), (1, psT)):
                    for r in range(2):
                        ch.done(v.bn_stats(st[:, 2 * c + r, :], src[:, r * HALF:(r + 1) * HALF]))
                ch.wait()
                for c in range(CT):
                    ch.done(v.bn_aggr(gs[:, c, 0:2], st[:, 2 * c:2 * c + 2, :].rearrange("p a b -> p (a b)")))
                ch.wait()
                ch.step(v.tensor_tensor(gs[:, :, 2], gs[:, :, 0], gs[:, :, 0], ALU.mult))
                v.tensor_tensor(gs[:, :, 1], gs[:, :, 1], gs[:, :, 2], ALU.add).then_inc(S["gstat_done"], 1)
                dve.wait_ge(S["gmm_done"], b + 1)
                ch.step(v.tensor_copy(gn[:, :, 0:2].rearrange("p c k -> p k c"),
                                      psV[:, 0:2 * CT].rearrange("p (k c) -> p k c", k=2)))
                ch.step(v.tensor_tensor(gn[:, :, 2], gn[:, :, 0], gn[:, :, 0], ALU.mult))
                ch.step(v.tensor_tensor(gn[:, :, 3], gn[:, :, 1], gn[:, :, 2], ALU.subtract))
                rstd(ch, dve, gn[:, :, 3], 1e-5, gn[:, :, 1], "gn_var", "gn_sq", b + 1)
                ch.step(v.tensor_tensor(gn[:, :, 1], gn[:, :, 1], par[:, 0, :], ALU.mult))
                ch.step(v.tensor_tensor(gn[:, :, 2], gn[:, :, 0], gn[:, :, 1], ALU.mult))
                ch.step(v.tensor_tensor(gn[:, :, 2], par[:, 1, :], gn[:, :, 2], ALU.subtract))
                wait(dve, "eo_done", 4 * b)
                ch.done(v.tensor_scalar(ab[:, :, 0], gn[:, :, 1], usc[:, 0:1], None, ALU.mult))
                v.tensor_scalar(ab[:, :, 1], gn[:, :, 2], usc[:, 0:1], None, ALU.mult).then_inc(S["ab_done"], 1)
                ch.end()

            def split(b):
                for q in range(3):
                    dve.wait_ge(S["uhi_done"], 3 * b + q + 1)
                    if q:
                        dve.wait_ge(S["diff_done"], 2 * b + q)
                    src = eo[:, :, 0, 1:SEQW] if q == 0 else diff[:, q - 1, :, 0:SEQW - 1]
                    v.tensor_tensor(U[:, 1, :, b, q, 0:SEQW - 1], src, U[:, 0, :, b, q, 0:SEQW - 1], ALU.subtract) \
                        .then_inc(S["ulo_done"], 1)

            def weights(kind, m):
                j = m % 3
                if kind == "wmax":
                    for c in range(CT):
                        dve.wait_ge(S[f"ws_in{c}"], 16 * (m + 1))
                        v.tensor_reduce(am[:, 4 + c:5 + c], wst[:, c].rearrange("p s k o -> p (s k o)"), X, ALU.max,
                                        apply_absolute_value=True).then_inc(S["c_m"], 1)
                if kind == "wscale":
                    ch = Chain(dve, "c_w", m, 4)
                    dve.wait_ge(S["c_m"], 2 * (m + 1))
                    v.tensor_tensor(am[:, 0:1], am[:, 4:5], am[:, 5:6], ALU.max).then_inc(S["wam_done"], 1)
                    dve.wait_ge(S["war_done"], m + 1)
                    pow2(ch, amr[:, 0:1], WK, wsc[:, 0, m:m + 1], wsc[:, 1, m:m + 1])
                    v.tensor_tensor(isc[:, m:m + 1], wsc[:, 1, m:m + 1], usc[:, 1:2], ALU.mult) \
                        .then_inc(S["wsc_done"], 1)
                    ch.end()
                if kind == "wsum":
                    for h in range(SUMS):
                        c, t = h // (SUMS // CT), h % (SUMS // CT) * SUM_TAPS
                        dve.wait_ge(S["whi_done"], PARTS * m + h + 1)
                        v.scalar_tensor_tensor(W[:, j, 1, c, 0, t:t + SUM_TAPS], wsum[:, h % 2],
                                               wsc[:, 0, m:m + 1], W[:, j, 0, c, 0, t:t + SUM_TAPS],
                                               ALU.mult, ALU.subtract).then_inc(S["wlo_done"], 1)
                if kind in ("w0", "w1"):
                    q = int(kind[1])
                    for c in range(CT):
                        dve.wait_ge(S["whi_done"], PARTS * m + SUMS + 2 * q + c + 1)
                        v.scalar_tensor_tensor(W[:, j, 1, c, 1 + q], wst[:, c, q], wsc[:, 0, m:m + 1],
                                               W[:, j, 0, c, 1 + q], ALU.mult, ALU.subtract) \
                            .then_inc(S["wlo_done"], 1)

            def extra(kind, k):
                if kind == "ln":
                    layer_norm(k)
                if kind == "gn":
                    group_norm(k)
                if kind == "split":
                    split(k)
                weights(kind, k)

            def scale_y(run, j, n):
                ch = Chain(dve, ("c_u", "c_y")[j > 0], n if j == 0 else 2 * n + j - 1, 4 if j == 0 else 5)
                dve.wait_ge(S["yar_done"], run + 1)
                if j == 0:
                    pow2(ch, amr[:, 2:3], QK, vscale[:, 0:1], ysc[:, 1:2])
                    v.tensor_copy(vsc[:, bass.ds(n, 1)], ysc[:, 1:2]).then_inc(S["ysc_done"], 1)
                else:
                    pow2(ch, amr[:, 2:3], QK, ysc[:, 0:1], ysc[:, 1:2])
                    ch.step(v.tensor_scalar(esc[:, j - 1, 0:1], ysc[:, 1:2], ysc[:, 1:2], D ** -0.5, ALU.mult, ALU.mult))
                    v.tensor_scalar(esc[:, j - 1, 1:2], esc[:, j - 1, 0:1], -1.0, None, ALU.mult) \
                        .then_inc(S["ysc_done"], 1)
                ch.end()

            def finish_y(n, p, j):
                y = yv if j == 0 else yqk
                dve.wait_ge(S["conv_done"], 9 * n + 3 * j + 3)
                dve.wait_ge(S["m_done"], 3 * n + j + 1)
                v.scalar_tensor_tensor(y[:, HALF:T], bank[2][:, :], isc[:, 3 * p + j:3 * p + j + 1], m_sb[:, :], ALU.mult,
                                       ALU.add).then_inc(S["y1_done"], 1)
                dve.wait_ge(S["y1_done"], 3 * n + j + 1)
                dve.wait_ge(S["y0_done"], 3 * n + j + 1)
                v.tensor_reduce(am[:, 2:3], y[:, :], X, ALU.max, apply_absolute_value=True).then_inc(S["yam_done"], 1)

            def qk_lo(run, hd, runs):
                ch = Chain(dve, "c_k", runs, 3)
                dve.wait_ge(S["qk_hi"], 2 * runs + 2)
                ch.done(v.scalar_tensor_tensor(stack[D:P, hd, 0, :], yqk[0:D, :], ysc[0:D, 0:1], stack[0:D, hd, 0, :],
                                               ALU.mult, ALU.subtract))
                ch.step(v.scalar_tensor_tensor(stack[D:P, hd, 2, :], yqk[D:P, :], ysc[D:P, 0:1], stack[D:P, hd, 1, :],
                                               ALU.mult, ALU.subtract))
                ch.step(v.tensor_copy(stack[0:D, hd, 1, :], stack[D:P, hd, 1, :]))
                v.tensor_copy(stack[0:D, hd, 2, :], stack[D:P, hd, 2, :]).then_inc(S["qk_done"], 1)
                ch.end()

            def project(b, i):
                q = 8 * b + i
                ch = Chain(dve, "c_x", q, 1)
                if i == 0:
                    dve.wait_ge(S["base_done"], b + 1)
                    wait(dve, "o_sum", b - 1)
                dve.wait_ge(S["pj_done"], q + 1)
                x = x1[:, b % 2, i, :]
                ch.step(v.scalar_tensor_tensor(x, bank[q % 3][:, 0:C], alpha[:, b:b + 1], base[:, b % 2, i, :],
                                               ALU.mult, ALU.add))
                v.scalar_tensor_tensor(x, bank[q % 3][:, C:2 * C], alpha[:, NB + b:NB + b + 1], x, ALU.mult, ALU.add) \
                    .then_inc(S["pj_used"], 1)
                ch.end()

            LF = 52
            chains = [Chain(dve, "c_f", b, LF) for b in range(NB)]

            def last_stage(kind, b):
                ch, stats, z = chains[b], ln[:, b], zz[:, b % 2]
                if kind == "nmr":
                    v.scalar_tensor_tensor(nmr[:, :, :], ln[:, :, :, 0], -1.0, ln[:, :, :, 1], ALU.mult, ALU.mult) \
                        .then_inc(S["nmr_done"], 1)
                if kind == "pw":
                    cp = Chain(dve, "c_p", 0, 4)
                    dve.wait_ge(S["pw_in"], 32)
                    v.tensor_reduce(am[:, 3:4], pws, X, ALU.max, apply_absolute_value=True).then_inc(S["pwam_done"], 1)
                    dve.wait_ge(S["pwar_done"], 1)
                    pow2(cp, amr[:, 3:4], PK, pwsc[:, 0:1], pwsc[:, 1:2])
                    v.tensor_scalar(alpha[:, :], vsc[:, :], pwsc[:, 1:2], None, ALU.mult).then_inc(S["pwsc_done"], 1)
                    cp.end()
                    dve.wait_ge(S["pwhi_done"], 1)
                    v.scalar_tensor_tensor(pw[:, 1].rearrange("p a k o -> p (a k o)"), pws, pwsc[:, 0:1],
                                           pw[:, 0].rearrange("p a k o -> p (a k o)"), ALU.mult, ALU.subtract) \
                        .then_inc(S["pw_done"], 1)
                if kind == "stats":
                    dve.wait_ge(S["pj_used"], 8 * (b + 1))
                    layer_norm_stats(ch, x1[:, b % 2], stats)
                if kind == "norm":
                    rstd(ch, dve, stats[:, :, 1], 1e-5, stats[:, :, 1], "f_var", "f_sq", b + 1)
                    v.scalar_tensor_tensor(nmr[:, b, :], stats[:, :, 0], -1.0, stats[:, :, 1], ALU.mult, ALU.mult) \
                        .then_inc(S["f_nm"], 1)
                score = tail[:, 0:3, :]
                mark, shl, shr, a1, a2 = (tail[:, 6 + q, :] for q in range(5))
                if kind == "find":
                    dve.wait_ge(S["zz_done"], 8 * (b + 1))
                    for w, off in enumerate((32, 40, 48)):
                        ch.step(v.scalar_tensor_tensor(hot, z[:, :, off:off + 16], 0.5,
                                                       ramp[:, 0:1, :].to_broadcast([P, 8, 16]), ALU.is_gt, ALU.mult))
                        ch.step(v.tensor_reduce(tail[:, w, :], hot, X, ALU.max))
                    ch.step(v.tensor_scalar(tail[:, 3:6, :], score, -1.0, 16.0, ALU.mult, ALU.add))
                    ch.step(v.scalar_tensor_tensor(tail[:, 3:6, :], score, 0.5, tail[:, 3:6, :], ALU.is_gt, ALU.mult))
                if kind == "shift":
                    lo, hi, sa = tail[:, 3, :], tail[:, 4, :], tail[:, 5, :]
                    for q, c in ((mark, 0), (shl, 39), (shr, 40)):
                        ch.done(v.tensor_scalar(q, z[:, :, c], 0.5, None, ALU.is_gt))
                    ch.done(v.scalar_tensor_tensor(taili[:, 0, :], hi, 16.0, lo, ALU.mult, ALU.add))
                    ch.step(v.tensor_copy(taili[:, 1, :], sa))
                    ch.done(v.tensor_tensor(a1, mark, shl, ALU.mult))
                    ch.done(v.tensor_tensor(taili[:, 2, :], taili[:, 0, :], taili[:, 1, :], ALU.logical_shift_left))
                    ch.step(v.tensor_tensor(taili[:, 3, :], taili[:, 0, :], taili[:, 1, :], ALU.logical_shift_right))
                    ch.done(v.tensor_tensor(mark, mark, a1, ALU.subtract))
                    ch.step(v.tensor_scalar(taili[:, 2, :], taili[:, 2, :], 255, None, ALU.bitwise_and))
                    ch.done(v.tensor_tensor(shl, taili[:, 2, :], a1, ALU.mult))
                    ch.step(v.tensor_tensor(a2, mark, shr, ALU.mult))
                    ch.step(v.tensor_tensor(shr, taili[:, 3, :], a2, ALU.mult))
                    ch.done(v.tensor_tensor(taili[:, 4, :], shl, shr, ALU.add))
                    ch.step(v.tensor_tensor(a1, a1, a2, ALU.add))
                    ch.done(v.tensor_scalar(taili[:, 5, :], taili[:, 4, :], 15, None, ALU.bitwise_and))
                    ch.step(v.tensor_scalar(taili[:, 6, :], taili[:, 4, :], 4, None, ALU.logical_shift_right))
                if kind == "mark":
                    digit = tail[:, 11:13, :]
                    for q in range(2):
                        ch.done(v.scalar_tensor_tensor(digit[:, q, :], taili[:, 5 + q, :], 1.0, a1, ALU.add, ALU.mult))
                    ch.wait()
                    ch.step(v.tensor_scalar(digit, digit, -1.0, None, ALU.add))
                    dve.wait_ge(S["o_sum"], b + 1)
                    for q, off in enumerate((64, 72)):
                        ch.step(v.tensor_tensor(hot, ramp[:, 1:2, :].to_broadcast([P, 8, 16]),
                                                digit[:, q, :].rearrange("p (i o) -> p i o", o=1)
                                                .to_broadcast([P, 8, 16]), ALU.is_equal))
                        w = ob[:, b % 2, :, off:off + 16]
                        last = v.scalar_tensor_tensor(w, hot, 2.0, w, ALU.mult, ALU.add)
                        if q == 0:
                            ch.step(last)
                        else:
                            last.then_inc(S["o_done"], 1)
                    ch.end()

            def step(n, p, b, attn, conv, more=None):
                k = n - 1
                for i in range(SLOTS if conv else LAST):
                    for kind, e in EXTRA.get(more, {}).get(i, []):
                        extra(kind, e)
                    if attn and i == 0:
                        vt = psT[:, :].rearrange("p (s h c) -> p s h c", s=8, h=2)
                        dve.wait_ge(S["vh_done"], 2 * k + 2)
                        for hd in range(2):
                            v.scalar_tensor_tensor(vT[:, :, hd, D * (1 - hd):D * (2 - hd)], vt[:, :, hd, :], vscale[:, 0:1],
                                                   vT[:, :, hd, D * hd:D * (hd + 1)], ALU.mult, ALU.subtract) \
                                .then_inc(S["vl_done"], 1)
                    if attn and i < UNITS:
                        u, hd = i, i // 8
                        ch = Chain(dve, "c_s", 16 * k + u, 2)
                        dve.wait_ge(S["s_done"], 16 * k + u + 1)
                        ch.step(v.reduce_max(smx[:, 0:1], psS[:, :], X))
                        v.tensor_scalar(smx[:, 1:2], smx[:, 0:1], esc[:, hd, 1:2], None, ALU.mult) \
                            .then_inc(S["nb_done"], 1)
                    if attn and 1 <= i <= UNITS:
                        u = i - 1
                        dve.wait_ge(S["ph_done"], 16 * k + u + 1)
                        v.tensor_tensor(probT[:, 1, :, u % 4 * P:(u % 4 + 1) * P],
                                        psT[:, :].rearrange("p (s t) -> p s t", s=8),
                                        probT[:, 0, :, u % 4 * P:(u % 4 + 1) * P], ALU.subtract) \
                            .then_inc(S["pl_done"], 1)
                    if attn and i < UNITS:
                        dve.wait_ge(S["e_done"], 16 * k + i + 1)
                        ch.step(v.reciprocal(smx[:, 3:4], smx[:, 2:3]))
                        v.tensor_scalar(prob, prob, smx[:, 3:4], 2.0 ** PROB_BITS, ALU.mult, ALU.mult) \
                            .then_inc(S["pn_done"], 1)
                        ch.end()
                    if attn and i == 0:
                        finish_y(k, pa(n, p), 2)
                    if attn and i == 1:
                        scale_y(3 * k + 2, 2, k)
                    if attn and i == 2:
                        qk_lo(3 * k + 2, 1, 2 * k + 1)
                    if conv and i in (4, 10, 16):
                        j = i // 6
                        dve.wait_ge(S["conv_done"], 9 * n + 3 * j + 2)
                        dve.wait_ge(S["m_done"], 3 * n + j + 1)
                        if j == 0:
                            wait(dve, "vt_done", n)
                        else:
                            wait(dve, "qk_hi", 4 * n + 2 * (j - 1))
                        y = yv if j == 0 else yqk
                        v.scalar_tensor_tensor(y[:, 0:HALF], bank[1][:, :], isc[:, 3 * p + j:3 * p + j + 1], m_sb[:, :],
                                               ALU.mult, ALU.add).then_inc(S["y0_done"], 1)
                    if conv and i in (6, 12):
                        finish_y(n, p, i // 6 - 1)
                    if conv and i in (7, 13):
                        scale_y(3 * n + i // 6 - 1, i // 6 - 1, n)
                    if conv and i == 14:
                        qk_lo(3 * n + 1, 0, 2 * n)
                    if attn and i in (5, 9, 13, 17):
                        gi = (i - 5) // 4
                        hd, r = gi // 2, gi % 2
                        R = D * hd
                        Hb = H[pa(n, p)]
                        dve.wait_ge(S["ht_done"], 4 * k + gi + 1)
                        v.scalar_tensor_tensor(hbuf[R:R + D, 1, :], psV[R:R + D, :], 2.0 ** -PROB_BITS,
                                               hbuf[R:R + D, 0, :], ALU.mult, ALU.add).then_inc(S["hs_done"], 1)
                        dve.wait_ge(S["hh_done"], 4 * k + gi + 1)
                        v.tensor_tensor(Hb[R:R + D, 1, ba(n, b), r, 1:1 + HALF], hbuf[R:R + D, 1, :],
                                        Hb[R:R + D, 0, ba(n, b), r, 1:1 + HALF], ALU.subtract).then_inc(S["hl_done"], 1)
                    if not conv:
                        for kind, e, t in LATE.get(i, []):
                            if kind == "tile":
                                project(e, t)
                            else:
                                last_stage(kind, e)

            dve.wait_ge(S["par_in"], 96)
            ch = Chain(dve, "c_b", 0, 6)
            ch.done(v.tensor_reduce(am[:, 4:5], par[:, 0, :], X, ALU.max, apply_absolute_value=True))
            ch.step(v.tensor_reduce(am[:, 5:6], par[:, 1, :], X, ALU.max, apply_absolute_value=True))
            v.tensor_scalar(am[:, 1:2], am[:, 4:5], (8.0 * T) ** 0.5, am[:, 5:6], ALU.mult, ALU.add) \
                .then_inc(S["bam_done"], 1)
            dve.wait_ge(S["bar_done"], 1)
            pow2(ch, amr[:, 1:2], UK, usc[:, 0:1], usc[:, 1:2])
            ch.end()
            for kind, e in EXTRA["start"][0]:
                extra(kind, e)
            step(0, 0, 0, False, True, 0)
            with dve.Fori(1, NB - 1) as n:
                step(n, 0, n, True, True)
            step(NB - 1, 0, NB - 1, True, True, NB - 1)
            step(NB, 1, 0, True, True, NB)
            with dve.Fori(NB + 1, STEPS) as n:
                step(n, 1, n - NB, True, True)
            step(STEPS, 2, 0, True, False)


def kernel(x, L0_conv_gn_gamma, L0_conv_gn_beta, L0_conv_qkv_w, L0_conv_qkv_b, L0_conv_proj_w, L0_conv_proj_b):
    import numpy as np
    import concourse.bacc as bacc
    from concourse.bass_utils import run_bass_kernel_spmd

    order = []
    for p in range(PAIRS):
        heads = (2 * p, 2 * p + 1)
        order += [3 * D * h + 2 * D + c for h in heads for c in range(D)]
        order += [3 * D * h + c for h in heads for c in range(2 * D)]
    order = np.array(order)
    x, wq, wp = np.asarray(x), np.asarray(L0_conv_qkv_w), np.asarray(L0_conv_proj_w)
    w = wq[order].reshape(6, P, CT, P, PH_TAPS, 2).transpose(0, 2, 3, 5, 4, 1).reshape(6, CT, P, TAPS * P)
    ident = np.eye(P, dtype=np.float32)
    group = np.kron(np.eye(P // 8, dtype=np.float32), np.full((8, 8), 0.125, np.float32))
    ramp = np.tile(np.concatenate([16 - np.arange(16), np.arange(16)]).astype(np.float32), (P, 1))
    data = {
        "x_tok": x.reshape(NB, C, T).transpose(0, 2, 1),
        "w_qkv": w,
        "b_qkv": np.asarray(L0_conv_qkv_b)[order].reshape(6, P).T,
        "gamma": np.asarray(L0_conv_gn_gamma).reshape(CT, P).T,
        "beta": np.asarray(L0_conv_gn_beta).reshape(CT, P).T,
        "w_proj": wp.reshape(C, PAIRS, P, PTAPS).transpose(2, 1, 3, 0).reshape(P, PAIRS * PTAPS * C),
        "b_proj": np.asarray(L0_conv_proj_b).reshape(1, C),
        "ident": ident, "group": group, "ramp": ramp,
    }
    nc = bacc.Bacc("TRN2", target_bir_lowering=False, num_devices=1)
    arrays, args = {}, []
    for name, a in data.items():
        arrays[name] = np.ascontiguousarray(a)
        args.append(nc.dram_tensor(name, a.shape, mybir.dt.from_np(a.dtype), kind="ExternalInput").ap())
    args.append(nc.dram_tensor("out_tok", (NB, T, C), F32, kind="ExternalOutput").ap())
    build(nc, *args)
    r = run_bass_kernel_spmd(nc, [arrays], core_ids=[0])
    out = np.asarray(r.results[0]["out_tok"])
    return np.ascontiguousarray(out.transpose(0, 2, 1)).reshape(NB, C, 32, 32)
```

```python
from contextlib import ExitStack

import concourse.bass as bass
from concourse import mybir

F32 = mybir.dt.float32
F16 = mybir.dt.float16
I32 = mybir.dt.int32
ALU = mybir.AluOpType
ACT = mybir.ActivationFunctionType
X = mybir.AxisListType.X
ABSMAX = bass.bass_isa.ReduceOp.absmax

P = 128
NB, T, C = 4, 1024, 256
CT = C // P
HALF = T // 2
TAPS, PTAPS = 16, 5
PH_TAPS = TAPS // 2
SUM_TAPS = 2
SUMS = CT * PH_TAPS // SUM_TAPS
PARTS = SUMS + 4
PAIRS, TILES = 2, 3
STEPS = PAIRS * NB
D = 64
UNITS = 16
SLOTS = 18
SEQW = HALF + PH_TAPS
HW = HALF + 2
LEFT = 4
EXP23 = float(1 << 23)
PROB_BITS = 13
WK, UK, QK, PK = 13, 13, 14, 14


def build(nc, x_tok, w_qkv, b_qkv, gamma, beta, w_proj, b_proj, ident_in, group_in, ramp_in, out_tok):
    with ExitStack() as ctx:
        def sb(name, shape, dt):
            return ctx.enter_context(nc.sbuf_tensor(name, shape, dt))

        def ps(name, shape):
            return ctx.enter_context(nc.psum_tensor(name, shape, F32))

        def sem(name):
            return ctx.enter_context(nc.semaphore(name))

        W = sb("W", [P, TILES, 2, CT, 3, PH_TAPS, P], F16)
        U = sb("U", [P, 2, CT, NB, 3, SEQW], F16)
        stack = sb("stack", [P, 2, 3, T], F16)
        yv = sb("yv", [P, T], F32)
        yqk = sb("yqk", [P, T], F32)
        m_sb = sb("m_sb", [P, HALF], F32)
        arena = sb("arena", [P, 5 * T], F32)
        prob = arena[:, 0:T]
        probT = arena[:, T:5 * T].bitcast(F16).rearrange("p (l s t) -> p l s t", l=2, s=8)
        eo = arena[:, 0:CT * 2 * SEQW].rearrange("p (c r w) -> p c r w", c=CT, r=2)
        diff = arena[:, CT * 2 * SEQW:2 * CT * 2 * SEQW].rearrange("p (d c w) -> p d c w", d=2, c=CT)
        vT = sb("vT", [P, 8, 2, P], F16)
        hbuf = sb("hbuf", [P, 2, HALF], F32)
        wsum = sb("wsum", [P, 2, SUM_TAPS, P], F32)
        H = [sb(f"H{p}", [P, 2, NB, 2, HW], F16) for p in range(PAIRS)]
        xs = H[0][:, :, :, :, :].rearrange("p a b r w -> p (a b r w)")[:, 0:8192].bitcast(F32) \
            .rearrange("p (n i c) -> p n i c", n=2, i=8)
        wst = H[1][:, :, :, :, :].rearrange("p a b r w -> p (a b r w)")[:, 0:8192].bitcast(F32) \
            .rearrange("p (c s k o) -> p c s k o", c=CT, s=2, k=PH_TAPS)
        ident = sb("ident_sb", [P, P], F32)
        group = sb("group_sb", [P, P], F32)
        ln = sb("ln", [P, NB, 8, 2], F32)
        st = sb("st", [P, 8, 6], F32)
        gs = sb("gs", [P, CT, 4], F32)
        gn = sb("gn", [P, CT, 4], F32)
        ab = sb("ab", [P, CT, 2], F32)
        nt = sb("nt", [P, 3, 8], F32)
        par = sb("par", [P, 2, CT], F32)
        qb = sb("qb", [P, 6], F32)
        am = sb("am", [P, 8], F32)
        amr = sb("amr", [P, 8], F32)
        bits = sb("bits", [P, 2], I32)
        usc = sb("usc", [P, 2], F32)
        wsc = sb("wsc", [P, 2, 6], F32)
        isc = sb("isc", [P, 6], F32)
        ysc = sb("ysc", [P, 2], F32)
        vsc = sb("vsc", [P, STEPS], F32)
        vscale = sb("vscale", [P, 1], F32)
        esc = sb("esc", [P, 2, 2], F32)
        smx = sb("smx", [P, 4], F32)
        Wf = W[:, :, :, :, :, :, :].rearrange("p a b c d e f -> p (a b c d e f)")
        Uf = U[:, :, :, :, :, :].rearrange("p a b c d e -> p (a b c d e)")
        PWN = PAIRS * PTAPS * C
        pws = Wf[:, 0:2 * PWN].bitcast(F32)
        pw = Wf[:, 2 * PWN:4 * PWN].rearrange("p (l a k o) -> p l a k o", l=2, a=PAIRS, k=PTAPS)
        WT = 2 * CT * 3 * PH_TAPS * P
        BUF = 2 * 2 * 8 * C
        pbb = Wf[:, 4 * PWN:4 * PWN + 2 * C].bitcast(F32)
        xf = Wf[:, WT:WT + BUF].bitcast(F32).rearrange("p (n i c) -> p n i c", n=2, i=8)
        base = Wf[:, 2 * WT - BUF // 2:2 * WT + BUF // 2].bitcast(F32).rearrange("p (n i c) -> p n i c", n=2, i=8)
        x1, ob = (Uf[:, q * BUF:(q + 1) * BUF].bitcast(F32).rearrange("p (n i c) -> p n i c", n=2, i=8) for q in range(2))
        small = Uf[:, 2 * BUF:2 * BUF + 2752].bitcast(F32)
        zz = small[:, 0:512].rearrange("p (i c) -> p i c", i=8)
        hot = small[:, 512:896].rearrange("p (i w k) -> p i w k", i=8, w=3)
        tail = small[:, 896:1152].rearrange("p (f i) -> p f i", i=8)
        taili = small[:, 1152:1280].bitcast(I32).rearrange("p (f i) -> p f i", i=8)
        xst = small[:, 1280:1376].rearrange("p (n i k) -> p n i k", n=2, i=8)
        ramp = sb("ramp_sb", [P, 2, 16], F32)
        alpha = sb("alpha", [P, STEPS], F32)
        nmr = sb("nmr", [P, NB, 8], F32)
        pwsc = sb("pwsc", [P, 2], F32)

        bank = [ps("cM", [P, HALF]), ps("cP", [P, HALF]), ps("cQ", [P, HALF])]
        psS = ps("psS", [P, T])
        psT = ps("psT", [P, T])
        psV = ps("psV", [P, HALF])

        names = """par_in pads x_in00 x_in01 x_in10 x_in11 z_done zT_done gstat_done gmm_done ab_done eo_done
            diff_done uhi_done first_hi first_lo ulo_done ln_sq ln_var gn_var gn_sq ws_in0 ws_in1 wam_done war_done
            wsc_done wsum_done whi_done wlo_done bam_done bar_done conv_done m_done y0_done y1_done yam_done
            yar_done ysc_done s_done nb_done e_done pn_done t_done ph_done pl_done pv_done ht_done hs_done hh_done
            hl_done z_nm bn_done pws_in vt_done vh_done vl_done qk_hi qk_done pw_in pwam_done pwar_done pwsc_done
            pwhi_done pw_done xf_in0 xf_in1 zf_done base_done pj_done pj_used f_var f_sq f_nm zz_done ob_done o_done
            out_sent0 out_sent1 last_sent c_a c_b c_g c_m c_w c_u c_y c_s c_k c_x c_f c_t c_p c_z""".split()
        S = {n: sem(n) for n in names}

        class Chain:
            def __init__(self, eng, name, run, per_run, start=None):
                self.eng, self.sem, self.per_run, self.n = eng, S[name], per_run, 0
                self.start = run * per_run if start is None else start

            def done(self, ins):
                ins.then_inc(self.sem, 1)
                self.n += 1

            def wait(self):
                self.eng.wait_ge(self.sem, self.start + self.n)

            def step(self, ins):
                self.done(ins)
                self.wait()

            def end(self):
                assert self.n == self.per_run, (self.sem, self.n, self.per_run)

        def pow2(ch, src, k, scale, inverse):
            v = nc.vector
            ch.step(v.tensor_scalar(inverse, src, 1e-30, None, ALU.max))
            ch.step(v.tensor_scalar(bits[:, 0:1], inverse.bitcast(I32), 0x7F800000, None, ALU.bitwise_and))
            ch.done(v.tensor_scalar(scale.bitcast(I32), bits[:, 0:1], -1.0, (254 + k) * EXP23, ALU.mult, ALU.add))
            ch.step(v.tensor_scalar(inverse.bitcast(I32), bits[:, 0:1], 1.0, -k * EXP23, ALU.mult, ALU.add))

        def rstd(ch, eng, var, eps, out, sq_asked, sq_done, runs):
            v = nc.vector
            n = nt[:, 0, 0:var.shape[-1]]
            s = nt[:, 1, 0:var.shape[-1]]
            q = nt[:, 2, 0:var.shape[-1]]
            v.tensor_scalar(n, var, eps, None, ALU.add).then_inc(S[sq_asked], 1)
            eng.wait_ge(S[sq_done], runs)
            ch.step(v.reciprocal(q, s))
            ch.step(v.tensor_tensor(s, n, q, ALU.mult))
            ch.step(v.tensor_tensor(s, s, q, ALU.mult))
            ch.step(v.tensor_scalar(s, s, -0.5, 1.5, ALU.mult, ALU.add))
            ch.step(v.tensor_tensor(out, q, s, ALU.mult))

        WSTAGES = ("wmax0", "wmax1", "wscale", "wsum0", "wsum1", "wsum2", "wsum3", "w00", "w01", "w10", "w11")

        def tile_weights(m, slots):
            return [(slot, (kind, m)) for slot, kind in zip(slots, WSTAGES)]

        def table(*lists):
            t = {}
            for slot, entry in sorted(sum(lists, []), key=lambda e: e[0]):
                t.setdefault(slot, []).append(entry)
            return t

        def batch_input(b, *slots):
            return [(slot, (kind, b)) for slot, kind in zip(slots, ("ln", "zT", "gstat", "gmm", "gn", "phase", "split"))]

        EXTRA = {
            0: table(batch_input(1, 0, 4, 4, 7, 7, 7, 10), tile_weights(1, (1, 1, 1, 2, 2, 2, 2, 2, 2, 2, 2)),
                     batch_input(2, 6, 10, 10, 13, 13, 13, 14), tile_weights(2, (8, 8, 8, 9, 9, 9, 9, 9, 9, 9, 9)),
                     batch_input(3, 13, 16, 15, 17, 17, 17, 17)),
            3: table(tile_weights(3, (1, 3, 4, 4, 5, 6, 8, 8, 9, 10, 10)), tile_weights(4, (12, 14, 15, 15, 16, 17, 17))),
            4: table(list(zip((1, 3, 4, 5), [(kind, 4) for kind in WSTAGES[7:]])),
                     tile_weights(5, (7, 8, 9, 9, 10, 11, 11, 12, 12, 14, 15)), [(16, ("pads", 0))]),
            STEPS - 1: {8: [("pwmax", 0)], 10: [("pwscale", 0)], 11: [("pw", 0)], 12: [("pw", 1)],
                        15: [("base", 0, 0), ("base", 0, 2)], 16: [("base", 0, 4), ("base", 0, 6)]},
        }
        START = {"vector": ("ln", "wmax0", "wmax1", "gstat", "wscale", "gn", "wsum0", "first0", "wsum1", "first1", "split",
                            "wsum2", "wsum3", "w00", "w01", "w10", "w11"),
                 "scalar": ("ln", "wsum0", "gn", "first0", "wsum1", "first1", "phase", "wsum2", "wsum3", "w00", "w01",
                            "split", "w10", "w11"),
                 "gpsimd": ("wmax0", "wmax1", "wsum1", "wsum2", "wsum3", "split")}
        RUNS = ((0, 0, 8), (1, 0, 8), (2, 0, 8), (3, 0, 4), (3, 4, 4))
        LATE = {}

        def late(slot, kind, b, *more):
            LATE.setdefault(slot, []).append((kind, b) + more)

        for b, slots in ((1, (2, 2, 3, 3)), (2, (7, 8, 9, 9)), (3, (12, 12, 14, 14))):
            for q, slot in enumerate(slots):
                late(slot, "base", b, 2 * q)
        halves = [2 if i in (0, 4, 8, 12, 15, 16) else 3 for i in range(SLOTS)]
        assert sum(halves) == 3 * 16
        beside = [i for i in range(SLOTS) for _ in range(halves[i])]
        for b in range(NB):
            for i in range(8):
                for p in range(PAIRS):
                    late(beside[16 * b + 2 * i + p] if b < 3 else SLOTS + i, "tile", b, i, p)
        run_slots = {"stats": (6, 14, 18, 23, 25), "norm": (6, 15, 18, 23, 25), "zz": (7, 16, 18, 23, 25)}
        ob_slots = ((7, 8, 9, 10), (16, 16, 17, 17), (18, 18, 19, 19), (23, 23), (25, 25))
        table_slots = {"find": (8, 17, 20, 25), "shift": (11, 17, 21, 25), "mark": (12, 17, 22, 25)}
        for run, (_, i0, _) in enumerate(RUNS):
            for kind, slots in run_slots.items():
                late(slots[run], kind, run)
            for q, slot in enumerate(ob_slots[run]):
                late(slot, "ob", run, i0 + 2 * q)
        for kind, slots in table_slots.items():
            for b in range(NB):
                late(slots[b], kind, b)
        LAST = max(LATE) + 1

        def is_int(v):
            return isinstance(v, int)

        def wait(eng, name, value):
            if not (is_int(value) and value <= 0):
                eng.wait_ge(S[name], value)

        def pa(n, p):
            return p - 1 if is_int(n) and n % NB == 0 else p

        def ba(n, b):
            return (n - 1) % NB if is_int(n) else b - 1

        block = ctx.enter_context(nc.Block())

        @block.sync
        def _(sp):
            xv = x_tok.rearrange("b (j p r) c -> b p j (r c)", j=4, r=2)
            ov = out_tok.rearrange("b (j p r) c -> b p j (r c)", j=4, r=2)

            def load_x(b):
                if b >= 2:
                    sp.wait_ge(S["zT_done"], b - 1)
                for h in range(2):
                    sp.dma_start(xs[:, b % 2, 4 * h:4 * h + 4, :].rearrange("p (j r) c -> p j (r c)", r=2),
                                 xv[b][:, 2 * h:2 * h + 2]).then_inc(S[f"x_in{b % 2}{h}"], 16)

            def load_w(m):
                if m >= 1:
                    sp.wait_ge(S["wlo_done"], PARTS * m)
                for c in range(CT):
                    sp.dma_start(wst[:, c].rearrange("p s k o -> p (s k o)"), w_qkv[m, c]).then_inc(S[f"ws_in{c}"], 16)

            load_x(0)
            for dst, src in ((par[:, 0, :], gamma), (par[:, 1, :], beta), (qb[:, :], b_qkv), (ident[:, :], ident_in),
                             (group[:, :], group_in), (ramp[:, :, :].rearrange("p a b -> p (a b)"), ramp_in)):
                sp.dma_start(dst, src).then_inc(S["par_in"], 16)
            load_w(0)
            load_x(1)
            load_w(1)
            load_x(2)
            load_w(2)
            load_x(3)
            for m in range(3, 6):
                load_w(m)
            sp.wait_ge(S["conv_done"], 9 * STEPS - 6)
            sp.dma_start(pws, w_proj).then_inc(S["pws_in"], 16)
            sp.dma_start(pbb, b_proj.to_broadcast([P, C])).then_inc(S["pw_in"], 16)
            sp.wait_ge(S["conv_done"], 9 * STEPS - 3)
            for b in range(NB):
                if b >= 2:
                    sp.wait_ge(S["base_done"], b - 1)
                sp.dma_start(xf[:, b % 2, :, :].rearrange("p (j r) c -> p j (r c)", r=2), xv[b]) \
                    .then_inc(S[f"xf_in{b % 2}"], 16)
            for b in range(NB):
                rows = ob[:, b % 2, :, :].rearrange("p (j r) c -> p j (r c)", r=2)
                if b < NB - 1:
                    sp.wait_ge(S["o_done"], b + 1)
                    sp.dma_start(ov[b], rows).then_inc(S[f"out_sent{b % 2}"], 16)
                else:
                    sp.wait_ge(S["ob_done"], 8 * NB)
                    for r in range(2):
                        sp.dma_start(ov[b][:, :, r * C + P:(r + 1) * C], rows[:, :, r * C + P:(r + 1) * C]) \
                            .then_inc(S["last_sent"], 16)
                    sp.wait_ge(S["o_done"], NB)
                    for r in range(2):
                        sp.dma_start(ov[b][:, :, r * C:r * C + P], rows[:, :, r * C:r * C + P]).then_inc(S["last_sent"], 16)
            sp.wait_ge(S["out_sent0"], 16 * 2)
            sp.wait_ge(S["out_sent1"], 16)
            sp.wait_ge(S["last_sent"], 16 * 4)

        @block.gpsimd
        def _(pool):
            g = nc.gpsimd

            def extra(kind, k, tile=None):
                if kind == "wmax1":
                    pool.wait_ge(S["wam_done"], k + 1)
                    g.partition_all_reduce(amr[:, 0:1], am[:, 0:1], P, ABSMAX).then_inc(S["war_done"], 1)
                if kind in ("wmax0", "wsum1", "wsum2", "wsum3"):
                    part = 0 if kind == "wmax0" else int(kind[4])
                    for h in range(part * SUMS // 4, (part + 1) * SUMS // 4):
                        c, t = h // (SUMS // CT), h % (SUMS // CT) * SUM_TAPS
                        wait(pool, "wlo_done", PARTS * k + h - 1 if h >= 2 else PARTS * (k - 1) + SUMS)
                        pool.wait_ge(S[f"ws_in{c}"], 16 * (k + 1))
                        g.tensor_tensor(wsum[:, h % 2], wst[:, c, 0, t:t + SUM_TAPS], wst[:, c, 1, t:t + SUM_TAPS],
                                        ALU.add).then_inc(S["wsum_done"], 1)
                if kind == "split":
                    seq = (eo[:, :, 0, 1:SEQW], diff[:, 0, :, 0:SEQW - 1], diff[:, 1, :, 0:SEQW - 1])

                    def difference(d):
                        if k != 1:
                            return
                        pool.wait_ge(S["eo_done"], 4 * (k + 1))
                        wait(pool, "ulo_done", 3 * k)
                        g.tensor_tensor(seq[1 + d], eo[:, :, 1, d:d + SEQW - 1], seq[0], ALU.subtract) \
                            .then_inc(S["diff_done"], 1)

                    def low(q):
                        if q:
                            pool.wait_ge(S["diff_done"], 2 * k + q)
                            pool.wait_ge(S["ulo_done"], 3 * k + q)
                        pool.wait_ge(S["eo_done"], 4 * k + 2)
                        pool.wait_ge(S["uhi_done"], 3 * k + q + 1)
                        g.tensor_tensor(U[:, 1, :, k, q, 0:SEQW - 1], seq[q], U[:, 0, :, k, q, 0:SEQW - 1],
                                        ALU.subtract).then_inc(S["ulo_done"], 1)

                    if k:
                        low(0)
                    difference(0)
                    difference(1)
                    low(1)
                    low(2)
                if kind == "pads":
                    pool.wait_ge(S["wlo_done"], 6 * PARTS)
                    for p in range(PAIRS):
                        for e in (0, HW - 1):
                            g.memset(H[p][:, :, :, :, e:e + 1].rearrange("p a b r w -> p (a b r) w"), 0.0) \
                                .then_inc(S["pads"], 1)

                if kind == "pwscale":
                    pool.wait_ge(S["pwam_done"], 1)
                    g.partition_all_reduce(amr[:, 3:4], am[:, 3:4], P, ABSMAX).then_inc(S["pwar_done"], 1)
                if kind == "base" and tile == 6:
                    pool.wait_ge(S["pw_in"], 16)
                    pool.wait_ge(S["zf_done"], 8 * (k + 1))
                    g.tensor_tensor(base[:, k % 2], base[:, k % 2], xf[:, k % 2], ALU.add).then_inc(S["c_z"], 1)
                    pool.wait_ge(S["c_z"], k + 1)
                    g.tensor_tensor(base[:, k % 2], base[:, k % 2], pbb[:, :].rearrange("p (o c) -> p o c", o=1)
                                    .to_broadcast([P, 8, C]), ALU.add).then_inc(S["base_done"], 1)

            def amax(run):
                pool.wait_ge(S["yam_done"], run + 1)
                g.tensor_tensor(am[:, 6:7], am[:, 2:3], ramp[:, 1, 1:2], ALU.mult)
                pool.drain()
                g.partition_all_reduce(amr[:, 2:3], am[:, 6:7], P, ABSMAX).then_inc(S["yar_done"], 1)

            pool.wait_ge(S["bam_done"], 1)
            g.partition_all_reduce(amr[:, 1:2], am[:, 1:2], P, ABSMAX).then_inc(S["bar_done"], 1)
            g.memset(eo[:, :, :, 0:LEFT], 0.0).then_inc(S["pads"], 1)
            g.memset(eo[:, :, :, LEFT + HALF:SEQW], 0.0).then_inc(S["pads"], 1)
            for kind in START["gpsimd"]:
                extra(kind, 0)

            def step(n, attn, more=None):
                for i in range(SLOTS):
                    for entry in EXTRA.get(more, {}).get(i, []):
                        extra(*entry)
                    if attn and i == 0:
                        amax(3 * n - 1)
                    if i == 6:
                        amax(3 * n)
                    if i == 12:
                        amax(3 * n + 1)

            step(0, False, 0)
            with pool.Fori(1, NB - 1) as n:
                step(n, True)
            step(NB - 1, True, NB - 1)
            step(NB, True, NB)
            with pool.Fori(NB + 1, STEPS - 1) as n:
                step(n, True)
            step(STEPS - 1, True, STEPS - 1)
            amax(3 * STEPS - 1)
            for i in range(LAST):
                for kind, b, *tile in LATE.get(i, []):
                    if kind == "base":
                        extra(kind, b, *tile)
                    if kind == "zz" and b < len(RUNS) - 1:
                        pool.wait_ge(S["f_nm"], b + 1)
                        b, i0, count = RUNS[b]
                        wait(pool, "o_done", b)
                        for t in range(i0, i0 + count):
                            g.tensor_scalar(zz[:, t, :], x1[:, b % 2, t, 0:64], ln[:, b, t, 1:2], nmr[:, b, t:t + 1],
                                            ALU.mult, ALU.add).then_inc(S["zz_done"], 1)

        @block.scalar
        def _(act):
            a = nc.scalar.activation

            def sqrt(asked, done, runs, width):
                act.wait_ge(S[asked], runs)
                a(nt[:, 1, 0:width], nt[:, 0, 0:width], ACT.Sqrt).then_inc(S[done], 1)

            def extra(kind, k, tile=None):
                j = k % 3

                if kind in ("pw", "base"):
                    last_stage(kind, k, tile)

                def phase(r):
                    for c, src in ((0, psS), (1, psT)):
                        a(eo[:, c, r, LEFT:LEFT + HALF], src[:, r * HALF:(r + 1) * HALF], ACT.Identity,
                          bias=ab[:, c, 1:2], scale=ab[:, c, 0:1]).then_inc(S["eo_done"], 1)

                if kind == "ln":
                    sqrt("ln_var", "ln_sq", k + 1, 8)
                    act.wait_ge(S["z_nm"], k + 1)
                    for i in range(8):
                        a(xs[:, k % 2, i, :], xs[:, k % 2, i, :], ACT.Identity, bias=nmr[:, k, i:i + 1],
                          scale=ln[:, k, i, 1:2]).then_inc(S["z_done"], 1)
                if kind == "gn":
                    sqrt("gn_var", "gn_sq", k + 1, CT)
                    act.wait_ge(S["ab_done"], k + 1)
                    act.wait_ge(S["pads"], 2)
                    wait(act, "ulo_done", 3 * k)
                    wait(act, "diff_done", 2 * k)
                    phase(0)
                if kind in ("first0", "first1"):
                    c = int(kind[5])
                    act.wait_ge(S["eo_done"], c + 1)
                    a(U[:, 0, c, 0, 0, 0:SEQW - 1], eo[:, c, 0, 1:SEQW], ACT.Copy) \
                        .then_inc(S[("first_hi", "uhi_done")[c]], 1)
                if kind == "phase":
                    phase(1)
                if kind == "split":
                    if k:
                        act.wait_ge(S["eo_done"], 4 * k + 2)
                        a(U[:, 0, :, k, 0, 0:SEQW - 1], eo[:, :, 0, 1:SEQW], ACT.Copy).then_inc(S["uhi_done"], 1)
                    for d in range(2):
                        act.wait_ge(S["diff_done"], 2 * k + d + 1)
                        a(U[:, 0, :, k, 1 + d, 0:SEQW - 1], diff[:, d, :, 0:SEQW - 1], ACT.Copy) \
                            .then_inc(S["uhi_done"], 1)
                    if k == NB - 1:
                        act.wait_ge(S["ulo_done"], 3 * k + 1)
                if kind.startswith("wsum") or kind in ("w00", "w01", "w10", "w11"):
                    act.wait_ge(S["wsc_done"], k + 1)
                    if k >= 3:
                        act.wait_ge(S["conv_done"], 27 + 3 * j + 1 + ("ws", "w0", "w1").index(kind[:2]))
                scale = wsc[:, 0, k:k + 1]
                if kind.startswith("wsum"):
                    for h in range(int(kind[4]) * SUMS // 4, (int(kind[4]) + 1) * SUMS // 4):
                        act.wait_ge(S["wsum_done"], SUMS * k + h + 1)
                        c, t = h // (SUMS // CT), h % (SUMS // CT) * SUM_TAPS
                        a(W[:, j, 0, c, 0, t:t + SUM_TAPS], wsum[:, h % 2], ACT.Copy, scale=scale) \
                            .then_inc(S["whi_done"], 1)
                if kind in ("w00", "w01", "w10", "w11"):
                    q, c = int(kind[1]), int(kind[2])
                    a(W[:, j, 0, c, 1 + q], wst[:, c, q], ACT.Copy, scale=scale).then_inc(S["whi_done"], 1)

            def qk_hi(run, hd, part):
                act.wait_ge(S["ysc_done"], run + 1)
                R = part * D
                a(stack[R:R + D, hd, part, :], yqk[R:R + D, :], ACT.Copy, scale=ysc[R:R + D, 0:1]).then_inc(S["qk_hi"], 1)

            def last_stage(kind, b, tile=None):
                if kind == "pw":
                    act.wait_ge(S["pwsc_done"], 1)
                    a(pw[:, 0, b].rearrange("p k o -> p (k o)"), pws[:, b * PWN // 2:(b + 1) * PWN // 2], ACT.Copy,
                      scale=pwsc[:, 0:1]).then_inc(S["pwhi_done"], 1)
                if kind == "base":
                    if tile == 0:
                        act.wait_ge(S[f"xf_in{b % 2}"], 16 * (b // 2 + 1))
                    if tile == 0 and b == 1:
                        act.wait_ge(S["conv_done"], 9 * STEPS)
                    if tile == 0 and b >= 2:
                        act.wait_ge(S["pj_used"], 8 * (b - 1))
                    for i in (tile, tile + 1):
                        a(base[:, b % 2, i, :], xf[:, b % 2, i, :], ACT.Identity, bias=nmr[:, b, i:i + 1],
                          scale=ln[:, b, i, 1:2]).then_inc(S["zf_done"], 1)
                if kind == "norm":
                    sqrt("f_var", "f_sq", b + 1, RUNS[b][2])
                if kind == "ob":
                    act.wait_ge(S["f_nm"], b + 1)
                    b = RUNS[b][0]
                    if b >= 2:
                        act.wait_ge(S[f"out_sent{b % 2}"], 16)
                    for i in (tile, tile + 1):
                        a(ob[:, b % 2, i, :], x1[:, b % 2, i, :], ACT.Identity, bias=nmr[:, b, i:i + 1],
                          scale=ln[:, b, i, 0:1]).then_inc(S["ob_done"], 1)

            def step(n, p, b, attn, conv, more=None):
                k = n - 1
                for i in range(SLOTS if conv else LAST):
                    for entry in EXTRA.get(more, {}).get(i, []):
                        extra(*entry)
                    if attn and i == 0:
                        act.wait_ge(S["vt_done"], k + 1)
                        act.wait_ge(S["ysc_done"], 3 * k + 1)
                        vt = psT[:, :].rearrange("p (s h c) -> p s h c", s=8, h=2)
                        a(vT[:, :, 0, 0:D], vt[:, :, 0, :], ACT.Copy, scale=vscale[:, 0:1]).then_inc(S["vh_done"], 1)
                        a(vT[:, :, 1, D:P], vt[:, :, 1, :], ACT.Copy, scale=vscale[:, 0:1]).then_inc(S["vh_done"], 1)
                    if attn and 1 <= i <= UNITS:
                        u = i - 1
                        act.wait_ge(S["t_done"], 16 * k + u + 1)
                        if u >= 4:
                            act.wait_ge(S["pv_done"], 4 * k + u // 4)
                        a(probT[:, 0, :, u % 4 * P:(u % 4 + 1) * P], psT[:, :].rearrange("p (s t) -> p s t", s=8),
                          ACT.Copy).then_inc(S["ph_done"], 1)
                    if attn and i < UNITS:
                        u, hd = i, i // 8
                        act.wait_ge(S["nb_done"], 16 * k + u + 1)
                        if u:
                            act.wait_ge(S["t_done"], 16 * k + u)
                        a(prob, psS[:, :], ACT.Exp, bias=smx[:, 1:2], scale=esc[:, hd, 0:1],
                          accum_out=smx[:, 2:3]).then_inc(S["e_done"], 1)
                    if conv and i in (2, 8, 14):
                        j = i // 6
                        act.wait_ge(S["conv_done"], 9 * n + 3 * j + 1)
                        wait(act, "y1_done", 3 * n + j)
                        a(m_sb[:, :], bank[0][:, :], ACT.Identity, bias=qb[:, 3 * p + j:3 * p + j + 1],
                          scale=isc[:, 3 * p + j:3 * p + j + 1]).then_inc(S["m_done"], 1)
                    if attn and i == 1:
                        qk_hi(3 * k + 2, 1, 0)
                        qk_hi(3 * k + 2, 1, 1)
                    if attn and i in (5, 9, 13, 17):
                        gi = (i - 5) // 4
                        hd, r = gi // 2, gi % 2
                        R, O = D * hd, D * (1 - hd)
                        act.wait_ge(S["pv_done"], 4 * k + gi + 1)
                        a(hbuf[R:R + D, 0, :], psV[O:O + D, :], ACT.Copy, scale=2.0 ** -PROB_BITS) \
                            .then_inc(S["ht_done"], 1)
                        act.wait_ge(S["hs_done"], 4 * k + gi + 1)
                        a(H[pa(n, p)][R:R + D, 0, ba(n, b), r, 1:1 + HALF], hbuf[R:R + D, 1, :], ACT.Copy) \
                            .then_inc(S["hh_done"], 1)
                    if conv and i in (13, 14):
                        qk_hi(3 * n + 1, 0, i - 13)
                    if not conv:
                        for entry in LATE.get(i, []):
                            last_stage(*entry[:3])

            for kind in START["scalar"]:
                extra(kind, 0)
            step(0, 0, 0, False, True, 0)
            with act.Fori(1, NB - 1) as n:
                step(n, 0, n, True, True)
            step(NB - 1, 0, NB - 1, True, True, NB - 1)
            step(NB, 1, 0, True, True, NB)
            with act.Fori(NB + 1, STEPS - 1) as n:
                step(n, 1, n - NB, True, True)
            step(STEPS - 1, 1, NB - 1, True, True, STEPS - 1)
            step(STEPS, 2, 0, True, False)

        @block.tensor
        def _(pe):
            mm, tr = nc.tensor.matmul, nc.tensor.transpose

            batch_reg = pe.alloc_register("batch")

            def fresh(b):
                if is_int(b):
                    return b
                pe.reg_mov(batch_reg, b)
                return pe.snap(batch_reg)

            def z_transpose(b):
                wait(pe, "eo_done", 4 * b)
                for i in range(8):
                    pe.wait_ge(S["z_done"], 8 * b + i + 1)
                    j, r = i // 2, i % 2
                    for c, dst in ((0, psS), (1, psT)):
                        last = tr(dst[:, r * HALF + j * P:r * HALF + (j + 1) * P], xs[:, b % 2, i, c * P:(c + 1) * P],
                                  ident[:, :])
                last.then_inc(S["zT_done"], 1)

            def group_mean(b):
                pe.wait_ge(S["gstat_done"], b + 1)
                mm(psV[:, 0:2 * CT], group[:, :], gs[:, :, 0:2].rearrange("p c k -> p k c"), start=True, stop=True) \
                    .then_inc(S["gmm_done"], 1)

            def project(b, i, p):
                q, (j, r) = 8 * b + i, (i // 2, i % 2)
                if i == 0 and p == 0:
                    pe.wait_ge(S["hl_done"], 4 * (NB + b + 1))
                if q == 0 and p == 0:
                    pe.wait_ge(S["pw_done"], PAIRS)
                    pe.wait_ge(S["pads"], 6)
                if p:
                    pass
                elif q < 3:
                    pe.wait_ge(S[("m_done", "y0_done", "y1_done")[q]], 3 * STEPS)
                else:
                    pe.wait_ge(S["pj_used"], q - 2)
                for t in range(PTAPS):
                    d = r + t - 2
                    col = 1 + d // 2 + j * P
                    for hl, wl in ((0, 0), (0, 1), (1, 0)):
                        last = mm(bank[q % 3][:, p * C:(p + 1) * C], H[p][:, hl, b, d % 2, col:col + P],
                                  pw[:, wl, p, t, :], start=(t == 0 and hl + wl == 0),
                                  stop=(t == PTAPS - 1 and hl == 1), skip_group_check=True)
                if p == PAIRS - 1:
                    last.then_inc(S["pj_done"], 1)

            def step(n, p, b, attn, conv, more=None):
                k = n - 1
                for i in range(SLOTS if conv else LAST):
                    for kind, e, *_ in EXTRA.get(more, {}).get(i, []):
                        if kind == "zT":
                            z_transpose(e)
                        if kind == "gmm":
                            group_mean(e)
                    if attn and i in (5, 9, 13, 17):
                        gi = (i - 5) // 4
                        hd = gi // 2
                        pe.wait_ge(S["pl_done"], 16 * k + 4 * gi + 4)
                        if gi == 0:
                            pe.wait_ge(S["vl_done"], 2 * k + 2)
                        if gi:
                            pe.wait_ge(S["hs_done"], 4 * k + gi)
                        for s in range(8):
                            for l in range(2):
                                last = mm(psV[:, :], vT[:, s, hd, :], probT[:, l, s, :], start=(s + l == 0),
                                          stop=(s + l == 8))
                        last.then_inc(S["pv_done"], 1)
                    if attn and 1 <= i <= UNITS:
                        u = i - 1
                        pe.wait_ge(S["pn_done"], 16 * k + u + 1)
                        if u == 0:
                            pe.wait_ge(S["ulo_done"], 3 * NB)
                            pe.wait_ge(S["vl_done"], 2 * k + 2)
                        else:
                            pe.wait_ge(S["pl_done"], 16 * k + u)
                        for s in range(8):
                            last = tr(psT[:, s * P:(s + 1) * P], prob[:, s * P:(s + 1) * P], ident[:, :])
                        last.then_inc(S["t_done"], 1)
                    if attn and i < UNITS:
                        u, hd = i, i // 8
                        if u % 8 == 0:
                            pe.wait_ge(S["qk_done"], 2 * k + hd + 1)
                        if u:
                            pe.wait_ge(S["e_done"], 16 * k + u)
                        for h in range(2):
                            for l in range(2):
                                last = mm(psS[:, h * HALF:(h + 1) * HALF], stack[:, hd, 0, u % 8 * P:(u % 8 + 1) * P],
                                          stack[:, hd, 1 + l, h * HALF:(h + 1) * HALF], start=(l == 0), stop=(l == 1))
                        last.then_inc(S["s_done"], 1)
                    if conv:
                        q = i // 2
                        j, kind = q // 3, q % 3
                        if i % 2 == 0:
                            wait(pe, ("m_done", "y0_done", "y1_done")[kind], 3 * n + j)
                            first = SUMS // 2 if more == 0 and i == 0 else 0
                            pe.wait_ge(S["wlo_done"], PARTS * (3 * p + j) + SUMS + 2 * kind - first)
                            if more == 0 and i == 0:
                                pe.wait_ge(S["first_lo"], 1)
                            elif more == 0 and i <= 4:
                                pe.wait_ge(S["ulo_done"], kind + 1)
                            elif i == 0 and is_int(p) and p == 0:
                                pe.wait_ge(S["ulo_done"], 3 * n + 3)
                        if more == 0 and i == 1:
                            pe.wait_ge(S["ulo_done"], 1)
                            pe.wait_ge(S["wlo_done"], SUMS)
                        c = i % 2
                        bb = fresh(b)
                        for t in range(PH_TAPS):
                            for wl, ul in ((0, 0), (0, 1), (1, 0)):
                                last = mm(bank[kind][:, :], W[:, j, wl, c, kind, t, :], U[:, ul, c, bb, kind, t:t + HALF],
                                          start=(c == 0 and t == 0 and wl + ul == 0),
                                          stop=(c == 1 and t == PH_TAPS - 1 and wl == 1))
                        if i % 2 == 1:
                            last.then_inc(S["conv_done"], 1)
                    if not conv:
                        for kind, e, *tile in LATE.get(i, []):
                            if kind == "tile":
                                project(e, *tile)
                if conv:
                    pe.wait_ge(S["y1_done"], 3 * n + 1)
                    if attn:
                        pe.wait_ge(S["pl_done"], 16 * n)
                    else:
                        pe.wait_ge(S["eo_done"], 4 * NB)
                    for s in range(8):
                        last = tr(psT[:, s * P:(s + 1) * P], yv[:, s * P:(s + 1) * P], ident[:, :])
                    last.then_inc(S["vt_done"], 1)

            pe.wait_ge(S["par_in"], 96)
            z_transpose(0)
            group_mean(0)
            step(0, 0, 0, False, True, 0)
            with pe.Fori(1, NB - 1) as n:
                step(n, 0, n, True, True)
            step(NB - 1, 0, NB - 1, True, True)
            step(NB, 1, 0, True, True)
            with pe.Fori(NB + 1, STEPS - 1) as n:
                step(n, 1, n - NB, True, True)
            step(STEPS - 1, 1, NB - 1, True, True)
            step(STEPS, 2, 0, True, False)

        @block.vector
        def _(dve):
            v = nc.vector

            def layer_norm(b):
                ch = Chain(dve, "c_a", b, 21)
                for i in range(8):
                    if i % 4 == 0:
                        dve.wait_ge(S[f"x_in{b % 2}{i // 4}"], 16 * (b // 2 + 1))
                    ch.done(v.bn_stats(st[:, i, :], xs[:, b % 2, i, :]))
                ch.wait()
                for i in range(8):
                    ch.done(v.bn_aggr(ln[:, b, i, :], st[:, i, :]))
                ch.wait()
                rstd(ch, dve, ln[:, b, :, 1], 1e-6, ln[:, b, :, 1], "ln_var", "ln_sq", b + 1)
                ch.end()
                v.scalar_tensor_tensor(nmr[:, b, :], ln[:, b, :, 0], -1.0, ln[:, b, :, 1], ALU.mult, ALU.mult) \
                    .then_inc(S["z_nm"], 1)

            group_chains = [Chain(dve, "c_g", b, 19) for b in range(NB)]

            def group_stats(b):
                ch = group_chains[b]
                dve.wait_ge(S["zT_done"], b + 1)
                for c, src in ((0, psS), (1, psT)):
                    for r in range(2):
                        ch.done(v.bn_stats(st[:, 2 * c + r, :], src[:, r * HALF:(r + 1) * HALF]))
                ch.wait()
                for c in range(CT):
                    ch.done(v.bn_aggr(gs[:, c, 0:2], st[:, 2 * c:2 * c + 2, :].rearrange("p a b -> p (a b)")))
                ch.wait()
                ch.step(v.tensor_tensor(gs[:, :, 2], gs[:, :, 0], gs[:, :, 0], ALU.mult))
                v.tensor_tensor(gs[:, :, 1], gs[:, :, 1], gs[:, :, 2], ALU.add).then_inc(S["gstat_done"], 1)

            def group_norm(b):
                ch = group_chains[b]
                dve.wait_ge(S["gmm_done"], b + 1)
                ch.step(v.tensor_copy(gn[:, :, 0:2].rearrange("p c k -> p k c"),
                                      psV[:, 0:2 * CT].rearrange("p (k c) -> p k c", k=2)))
                ch.step(v.tensor_tensor(gn[:, :, 2], gn[:, :, 0], gn[:, :, 0], ALU.mult))
                ch.step(v.tensor_tensor(gn[:, :, 3], gn[:, :, 1], gn[:, :, 2], ALU.subtract))
                rstd(ch, dve, gn[:, :, 3], 1e-5, gn[:, :, 1], "gn_var", "gn_sq", b + 1)
                ch.step(v.tensor_tensor(gn[:, :, 1], gn[:, :, 1], par[:, 0, :], ALU.mult))
                ch.step(v.tensor_tensor(gn[:, :, 2], gn[:, :, 0], gn[:, :, 1], ALU.mult))
                ch.step(v.tensor_tensor(gn[:, :, 2], par[:, 1, :], gn[:, :, 2], ALU.subtract))
                wait(dve, "eo_done", 4 * b)
                ch.done(v.tensor_scalar(ab[:, :, 0], gn[:, :, 1], usc[:, 0:1], None, ALU.mult))
                v.tensor_scalar(ab[:, :, 1], gn[:, :, 2], usc[:, 0:1], None, ALU.mult).then_inc(S["ab_done"], 1)
                ch.end()

            def weights(kind, m):
                j = m % 3
                if kind in ("wmax0", "wmax1"):
                    c = int(kind[4])
                    dve.wait_ge(S[f"ws_in{c}"], 16 * (m + 1))
                    v.tensor_reduce(am[:, 4 + c:5 + c], wst[:, c].rearrange("p s k o -> p (s k o)"), X, ALU.max,
                                    apply_absolute_value=True).then_inc(S["c_m"], 1)
                if kind == "wmax1":
                    dve.wait_ge(S["c_m"], 2 * (m + 1))
                    v.tensor_tensor(am[:, 0:1], am[:, 4:5], am[:, 5:6], ALU.max).then_inc(S["wam_done"], 1)
                if kind == "wscale":
                    ch = Chain(dve, "c_w", m, 4)
                    dve.wait_ge(S["war_done"], m + 1)
                    pow2(ch, amr[:, 0:1], WK, wsc[:, 0, m:m + 1], wsc[:, 1, m:m + 1])
                    v.tensor_tensor(isc[:, m:m + 1], wsc[:, 1, m:m + 1], usc[:, 1:2], ALU.mult) \
                        .then_inc(S["wsc_done"], 1)
                    ch.end()
                if kind.startswith("wsum"):
                    for h in range(int(kind[4]) * SUMS // 4, (int(kind[4]) + 1) * SUMS // 4):
                        c, t = h // (SUMS // CT), h % (SUMS // CT) * SUM_TAPS
                        dve.wait_ge(S["whi_done"], PARTS * m + h + 1)
                        v.scalar_tensor_tensor(W[:, j, 1, c, 0, t:t + SUM_TAPS], wsum[:, h % 2],
                                               wsc[:, 0, m:m + 1], W[:, j, 0, c, 0, t:t + SUM_TAPS],
                                               ALU.mult, ALU.subtract).then_inc(S["wlo_done"], 1)
                if kind in ("w00", "w01", "w10", "w11"):
                    q, c = int(kind[1]), int(kind[2])
                    dve.wait_ge(S["whi_done"], PARTS * m + SUMS + 2 * q + c + 1)
                    v.scalar_tensor_tensor(W[:, j, 1, c, 1 + q], wst[:, c, q], wsc[:, 0, m:m + 1],
                                           W[:, j, 0, c, 1 + q], ALU.mult, ALU.subtract).then_inc(S["wlo_done"], 1)

            def extra(kind, k, tile=None):
                if kind == "split" and k != 1:
                    dve.wait_ge(S["eo_done"], 4 * (k + 1))
                    wait(dve, "ulo_done", 3 * k)
                    for d in range(2):
                        v.tensor_tensor(diff[:, d, :, 0:SEQW - 1], eo[:, :, 1, d:d + SEQW - 1], eo[:, :, 0, 1:SEQW],
                                        ALU.subtract).then_inc(S["diff_done"], 1)
                if kind == "ln":
                    layer_norm(k)
                if kind == "gstat":
                    group_stats(k)
                if kind == "gn":
                    group_norm(k)
                if kind in ("first0", "first1"):
                    c = int(kind[5])
                    dve.wait_ge(S[("first_hi", "uhi_done")[c]], 1)
                    v.tensor_tensor(U[:, 1, c, 0, 0, 0:SEQW - 1], eo[:, c, 0, 1:SEQW], U[:, 0, c, 0, 0, 0:SEQW - 1],
                                    ALU.subtract).then_inc(S[("first_lo", "ulo_done")[c]], 1)
                if kind in ("pwmax", "pwscale"):
                    last_stage(kind, k)
                if kind == "pw":
                    proj_low(k)
                weights(kind, k)

            def scale_y(run, j, n):
                ch = Chain(dve, ("c_u", "c_y")[j > 0], n if j == 0 else 2 * n + j - 1, 4 if j == 0 else 5)
                dve.wait_ge(S["yar_done"], run + 1)
                if j == 0:
                    pow2(ch, amr[:, 2:3], QK, vscale[:, 0:1], ysc[:, 1:2])
                    v.tensor_copy(vsc[:, bass.ds(n, 1)], ysc[:, 1:2]).then_inc(S["ysc_done"], 1)
                else:
                    pow2(ch, amr[:, 2:3], QK, ysc[:, 0:1], ysc[:, 1:2])
                    ch.step(v.tensor_scalar(esc[:, j - 1, 0:1], ysc[:, 1:2], ysc[:, 1:2], D ** -0.5, ALU.mult, ALU.mult))
                    v.tensor_scalar(esc[:, j - 1, 1:2], esc[:, j - 1, 0:1], -1.0, None, ALU.mult) \
                        .then_inc(S["ysc_done"], 1)
                ch.end()

            def finish_y(n, p, j):
                y = yv if j == 0 else yqk
                dve.wait_ge(S["conv_done"], 9 * n + 3 * j + 3)
                dve.wait_ge(S["m_done"], 3 * n + j + 1)
                v.scalar_tensor_tensor(y[:, HALF:T], bank[2][:, :], isc[:, 3 * p + j:3 * p + j + 1], m_sb[:, :], ALU.mult,
                                       ALU.add).then_inc(S["y1_done"], 1)
                dve.wait_ge(S["y1_done"], 3 * n + j + 1)
                dve.wait_ge(S["y0_done"], 3 * n + j + 1)
                v.tensor_reduce(am[:, 2:3], y[:, :], X, ALU.max, apply_absolute_value=True).then_inc(S["yam_done"], 1)

            def qk_lo(part, hd, runs):
                ch = Chain(dve, "c_k", runs, 3)
                ch.n = part
                if part == 0:
                    dve.wait_ge(S["qk_hi"], 2 * runs + 1)
                    ch.done(v.scalar_tensor_tensor(stack[D:P, hd, 0, :], yqk[0:D, :], ysc[0:D, 0:1], stack[0:D, hd, 0, :],
                                                   ALU.mult, ALU.subtract))
                if part == 1:
                    dve.wait_ge(S["qk_hi"], 2 * runs + 2)
                    ch.done(v.scalar_tensor_tensor(stack[D:P, hd, 2, :], yqk[D:P, :], ysc[D:P, 0:1], stack[D:P, hd, 1, :],
                                                   ALU.mult, ALU.subtract))
                if part == 2:
                    ch.wait()
                    ch.step(v.tensor_copy(stack[0:D, hd, 1, :], stack[D:P, hd, 1, :]))
                    v.tensor_copy(stack[0:D, hd, 2, :], stack[D:P, hd, 2, :]).then_inc(S["qk_done"], 1)
                    ch.end()

            def tile_stats(b, i):
                dve.wait_ge(S["pj_used"], 8 * b + i + 1)
                v.bn_stats(xst[:, b % 2, i, :], x1[:, b % 2, i, :]).then_inc(S["bn_done"], 1)

            def project(b, i):
                q = 8 * b + i
                ch = Chain(dve, "c_x", q, 1)
                if i == 0:
                    dve.wait_ge(S["base_done"], b + 1)
                    wait(dve, "ob_done", 8 * (b - 1))
                    wait(dve, "zz_done", 8 * (b - 1))
                dve.wait_ge(S["pj_done"], q + 1)
                x = x1[:, b % 2, i, :]
                ch.step(v.scalar_tensor_tensor(x, bank[q % 3][:, 0:C], alpha[:, b:b + 1], base[:, b % 2, i, :],
                                               ALU.mult, ALU.add))
                v.scalar_tensor_tensor(x, bank[q % 3][:, C:2 * C], alpha[:, NB + b:NB + b + 1], x, ALU.mult, ALU.add) \
                    .then_inc(S["pj_used"], 1)
                ch.end()
                if q:
                    tile_stats((q - 1) // 8, (q - 1) % 8)

            results = [6 + count for _, _, count in RUNS]
            runs = [Chain(dve, "c_f", None, results[q], sum(results[:q])) for q in range(len(RUNS))]
            tables = [Chain(dve, "c_t", b, 29) for b in range(NB)]

            def proj_low(p):
                dve.wait_ge(S["pwhi_done"], p + 1)
                v.scalar_tensor_tensor(pw[:, 1, p].rearrange("p k o -> p (k o)"), pws[:, p * PWN // 2:(p + 1) * PWN // 2],
                                       pwsc[:, 0:1], pw[:, 0, p].rearrange("p k o -> p (k o)"), ALU.mult, ALU.subtract) \
                    .then_inc(S["pw_done"], 1)

            def last_stage(kind, run):
                if kind == "pwmax":
                    dve.wait_ge(S["pws_in"], 16)
                    v.tensor_reduce(am[:, 3:4], pws, X, ALU.max, apply_absolute_value=True).then_inc(S["pwam_done"], 1)
                if kind == "pwscale":
                    cp = Chain(dve, "c_p", 0, 4)
                    dve.wait_ge(S["pwar_done"], 1)
                    pow2(cp, amr[:, 3:4], PK, pwsc[:, 0:1], pwsc[:, 1:2])
                    v.tensor_scalar(alpha[:, :], vsc[:, :], pwsc[:, 1:2], None, ALU.mult).then_inc(S["pwsc_done"], 1)
                    cp.end()
                if kind in ("stats", "norm", "zz"):
                    ch, (b, i0, count) = runs[run], RUNS[run]
                    stats = ln[:, b, i0:i0 + count]
                if kind == "stats":
                    if run == len(RUNS) - 1:
                        tile_stats(b, 7)
                    dve.wait_ge(S["bn_done"], 8 * b + i0 + count)
                    for i in range(i0, i0 + count):
                        ch.done(v.bn_aggr(ln[:, b, i, :], xst[:, b % 2, i, :]))
                    ch.wait()
                if kind == "norm":
                    rstd(ch, dve, stats[:, :, 1], 1e-5, stats[:, :, 1], "f_var", "f_sq", run + 1)
                    ch.step(v.scalar_tensor_tensor(nmr[:, b, i0:i0 + count], stats[:, :, 0], -1.0, stats[:, :, 1], ALU.mult,
                                                   ALU.mult))
                    v.tensor_scalar(stats[:, :, 0], stats[:, :, 1], 1.0, None, ALU.add).then_inc(S["f_nm"], 1)
                    ch.end()
                if kind == "zz" and run == len(RUNS) - 1:
                    dve.wait_ge(S["f_nm"], run + 1)
                    for t in range(i0, i0 + count):
                        v.tensor_scalar(zz[:, t, :], x1[:, b % 2, t, 0:64], ln[:, b, t, 1:2], nmr[:, b, t:t + 1], ALU.mult,
                                        ALU.add).then_inc(S["zz_done"], 1)
                if kind in ("find", "shift", "mark"):
                    ch, b = tables[run], run
                    score, found = tail[:, 0:3, :], tail[:, 3:6, :]
                    mark, shl, shr, a1, a2 = (tail[:, 6 + q, :] for q in range(5))
                    value, by, left, right, both, low_digit, high_digit = (taili[:, q, :] for q in range(7))
                if kind == "find":
                    dve.wait_ge(S["zz_done"], 8 * (b + 1))
                    for w, off in enumerate((32, 40, 48)):
                        ch.done(v.scalar_tensor_tensor(hot[:, :, w, :], zz[:, :, off:off + 16], 0.5,
                                                       ramp[:, 0:1, :].to_broadcast([P, 8, 16]), ALU.is_gt, ALU.mult))
                    ch.wait()
                    ch.step(v.tensor_reduce(score.rearrange("p w i -> p i w"), hot[:, :], X, ALU.max))
                    ch.step(v.tensor_scalar(found, score, -1.0, 16.0, ALU.mult, ALU.add))
                    ch.step(v.scalar_tensor_tensor(found, score, 0.5, found, ALU.is_gt, ALU.mult))
                if kind == "shift":
                    for q, c in ((mark, 0), (shl, 39), (shr, 40)):
                        ch.done(v.tensor_scalar(q, zz[:, :, c], 0.5, None, ALU.is_gt))
                    ch.done(v.scalar_tensor_tensor(value, found[:, 1, :], 16.0, found[:, 0, :], ALU.mult, ALU.add))
                    ch.step(v.tensor_copy(by, found[:, 2, :]))
                    ch.done(v.tensor_tensor(a1, mark, shl, ALU.mult))
                    ch.done(v.tensor_tensor(left, value, by, ALU.logical_shift_left))
                    ch.step(v.tensor_tensor(right, value, by, ALU.logical_shift_right))
                    ch.done(v.tensor_tensor(mark, mark, a1, ALU.subtract))
                    ch.step(v.tensor_scalar(left, left, 255, None, ALU.bitwise_and))
                    ch.done(v.tensor_tensor(shl, left, a1, ALU.mult))
                    ch.step(v.tensor_tensor(a2, mark, shr, ALU.mult))
                    ch.step(v.tensor_tensor(shr, right, a2, ALU.mult))
                    ch.done(v.tensor_tensor(both, shl, shr, ALU.add))
                    ch.step(v.tensor_tensor(a1, a1, a2, ALU.add))
                    ch.done(v.tensor_scalar(low_digit, both, 15, None, ALU.bitwise_and))
                    ch.step(v.tensor_scalar(high_digit, both, 4, None, ALU.logical_shift_right))
                if kind == "mark":
                    digit = tail[:, 11:13, :]
                    for q in range(2):
                        ch.done(v.scalar_tensor_tensor(digit[:, q, :], (low_digit, high_digit)[q], 1.0, a1, ALU.add, ALU.mult))
                    ch.wait()
                    ch.step(v.tensor_scalar(digit, digit, -1.0, None, ALU.add))
                    dve.wait_ge(S["ob_done"], 8 * (b + 1))
                    for q, off in enumerate((64, 72)):
                        ch.step(v.tensor_tensor(hot[:, :, 0, :], ramp[:, 1:2, :].to_broadcast([P, 8, 16]),
                                                digit[:, q, :].rearrange("p (i o) -> p i o", o=1)
                                                .to_broadcast([P, 8, 16]), ALU.is_equal))
                        w = ob[:, b % 2, :, off:off + 16]
                        last = v.scalar_tensor_tensor(w, hot[:, :, 0, :], 2.0, w, ALU.mult, ALU.add)
                        if q == 0:
                            ch.step(last)
                        else:
                            last.then_inc(S["o_done"], 1)
                    ch.end()

            def step(n, p, b, attn, conv, more=None):
                k = n - 1
                for i in range(SLOTS if conv else LAST):
                    for entry in EXTRA.get(more, {}).get(i, []):
                        extra(*entry)
                    if attn and i < UNITS:
                        u, hd = i, i // 8
                        ch = Chain(dve, "c_s", 16 * k + u, 2)
                        dve.wait_ge(S["s_done"], 16 * k + u + 1)
                        ch.step(v.reduce_max(smx[:, 0:1], psS[:, :], X))
                        v.tensor_scalar(smx[:, 1:2], smx[:, 0:1], esc[:, hd, 1:2], None, ALU.mult) \
                            .then_inc(S["nb_done"], 1)
                    if attn and i == 0:
                        vt = psT[:, :].rearrange("p (s h c) -> p s h c", s=8, h=2)
                        dve.wait_ge(S["vh_done"], 2 * k + 2)
                        for hd in range(2):
                            v.scalar_tensor_tensor(vT[:, :, hd, D * (1 - hd):D * (2 - hd)], vt[:, :, hd, :], vscale[:, 0:1],
                                                   vT[:, :, hd, D * hd:D * (hd + 1)], ALU.mult, ALU.subtract) \
                                .then_inc(S["vl_done"], 1)
                    if attn and 1 <= i <= UNITS:
                        u = i - 1
                        dve.wait_ge(S["ph_done"], 16 * k + u + 1)
                        v.tensor_tensor(probT[:, 1, :, u % 4 * P:(u % 4 + 1) * P],
                                        psT[:, :].rearrange("p (s t) -> p s t", s=8),
                                        probT[:, 0, :, u % 4 * P:(u % 4 + 1) * P], ALU.subtract) \
                            .then_inc(S["pl_done"], 1)
                    if attn and i < UNITS:
                        dve.wait_ge(S["e_done"], 16 * k + i + 1)
                        ch.step(v.reciprocal(smx[:, 3:4], smx[:, 2:3]))
                        v.tensor_scalar(prob, prob, smx[:, 3:4], 2.0 ** PROB_BITS, ALU.mult, ALU.mult) \
                            .then_inc(S["pn_done"], 1)
                        ch.end()
                    if attn and i == 0:
                        finish_y(k, pa(n, p), 2)
                    if attn and i == 1:
                        scale_y(3 * k + 2, 2, k)
                    if attn and i in (2, 3, 4):
                        qk_lo(i - 2, 1, 2 * k + 1)
                    if conv and i in (4, 10, 16):
                        j = i // 6
                        dve.wait_ge(S["conv_done"], 9 * n + 3 * j + 2)
                        dve.wait_ge(S["m_done"], 3 * n + j + 1)
                        if j == 0:
                            wait(dve, "vt_done", n)
                        else:
                            wait(dve, "qk_hi", 4 * n + 2 * (j - 1))
                        y = yv if j == 0 else yqk
                        v.scalar_tensor_tensor(y[:, 0:HALF], bank[1][:, :], isc[:, 3 * p + j:3 * p + j + 1], m_sb[:, :],
                                               ALU.mult, ALU.add).then_inc(S["y0_done"], 1)
                    if conv and i in (6, 12):
                        finish_y(n, p, i // 6 - 1)
                    if conv and i in (7, 13):
                        scale_y(3 * n + i // 6 - 1, i // 6 - 1, n)
                    if conv and i in (14, 15):
                        qk_lo(i - 14, 0, 2 * n)
                    if conv and i == 15:
                        qk_lo(2, 0, 2 * n)
                    if attn and i in (5, 9, 13, 17):
                        gi = (i - 5) // 4
                        hd, r = gi // 2, gi % 2
                        R = D * hd
                        Hb = H[pa(n, p)]
                        dve.wait_ge(S["ht_done"], 4 * k + gi + 1)
                        v.scalar_tensor_tensor(hbuf[R:R + D, 1, :], psV[R:R + D, :], 2.0 ** -PROB_BITS,
                                               hbuf[R:R + D, 0, :], ALU.mult, ALU.add).then_inc(S["hs_done"], 1)
                        dve.wait_ge(S["hh_done"], 4 * k + gi + 1)
                        v.tensor_tensor(Hb[R:R + D, 1, ba(n, b), r, 1:1 + HALF], hbuf[R:R + D, 1, :],
                                        Hb[R:R + D, 0, ba(n, b), r, 1:1 + HALF], ALU.subtract).then_inc(S["hl_done"], 1)
                    if not conv:
                        for kind, e, *tile in LATE.get(i, []):
                            if kind not in ("tile", "base", "ob"):
                                last_stage(kind, e)
                            elif kind == "tile" and tile[1] == PAIRS - 1:
                                project(e, tile[0])

            extra("ln", 0)
            dve.wait_ge(S["par_in"], 96)
            ch = Chain(dve, "c_b", 0, 6)
            ch.done(v.tensor_reduce(am[:, 1:2], par[:, 0, :], X, ALU.max, apply_absolute_value=True))
            ch.step(v.tensor_reduce(am[:, 7:8], par[:, 1, :], X, ALU.max, apply_absolute_value=True))
            v.tensor_scalar(am[:, 1:2], am[:, 1:2], (8.0 * T) ** 0.5, am[:, 7:8], ALU.mult, ALU.add) \
                .then_inc(S["bam_done"], 1)
            extra("wmax0", 0)
            dve.wait_ge(S["bar_done"], 1)
            pow2(ch, amr[:, 1:2], UK, usc[:, 0:1], usc[:, 1:2])
            ch.end()
            for kind in START["vector"][2:]:
                extra(kind, 0)
            step(0, 0, 0, False, True, 0)
            with dve.Fori(1, NB - 1) as n:
                step(n, 0, n, True, True)
            step(NB - 1, 0, NB - 1, True, True, NB - 1)
            step(NB, 1, 0, True, True, NB)
            with dve.Fori(NB + 1, STEPS - 1) as n:
                step(n, 1, n - NB, True, True)
            step(STEPS - 1, 1, NB - 1, True, True, STEPS - 1)
            step(STEPS, 2, 0, True, False)


def kernel(x, L0_conv_gn_gamma, L0_conv_gn_beta, L0_conv_qkv_w, L0_conv_qkv_b, L0_conv_proj_w, L0_conv_proj_b):
    import numpy as np
    import concourse.bacc as bacc
    from concourse.bass_utils import run_bass_kernel_spmd

    order = []
    for p in range(PAIRS):
        heads = (2 * p, 2 * p + 1)
        order += [3 * D * h + 2 * D + c for h in heads for c in range(D)]
        order += [3 * D * h + c for h in heads for c in range(2 * D)]
    order = np.array(order)
    x, wq, wp = np.asarray(x), np.asarray(L0_conv_qkv_w), np.asarray(L0_conv_proj_w)
    w = wq[order].reshape(6, P, CT, P, PH_TAPS, 2).transpose(0, 2, 3, 5, 4, 1).reshape(6, CT, P, TAPS * P)
    ident = np.eye(P, dtype=np.float32)
    group = np.kron(np.eye(P // 8, dtype=np.float32), np.full((8, 8), 0.125, np.float32))
    ramp = np.tile(np.concatenate([16 - np.arange(16), np.arange(16)]).astype(np.float32), (P, 1))
    data = {
        "x_tok": x.reshape(NB, C, T).transpose(0, 2, 1),
        "w_qkv": w,
        "b_qkv": np.asarray(L0_conv_qkv_b)[order].reshape(6, P).T,
        "gamma": np.asarray(L0_conv_gn_gamma).reshape(CT, P).T,
        "beta": np.asarray(L0_conv_gn_beta).reshape(CT, P).T,
        "w_proj": wp.reshape(C, PAIRS, P, PTAPS).transpose(2, 1, 3, 0).reshape(P, PAIRS * PTAPS * C),
        "b_proj": np.asarray(L0_conv_proj_b).reshape(1, C),
        "ident": ident, "group": group, "ramp": ramp,
    }
    nc = bacc.Bacc("TRN2", target_bir_lowering=False, num_devices=1)
    arrays, args = {}, []
    for name, a in data.items():
        arrays[name] = np.ascontiguousarray(a)
        args.append(nc.dram_tensor(name, a.shape, mybir.dt.from_np(a.dtype), kind="ExternalInput").ap())
    args.append(nc.dram_tensor("out_tok", (NB, T, C), F32, kind="ExternalOutput").ap())
    build(nc, *args)
    r = run_bass_kernel_spmd(nc, [arrays], core_ids=[0])
    out = np.asarray(r.results[0]["out_tok"])
    return np.ascontiguousarray(out.transpose(0, 2, 1)).reshape(NB, C, 32, 32)
```
